# Optimizing a Trainium2 kernel written in Bass

```python
import numpy as np
import jax
import jax.numpy as jnp

def _softmax(x, axis=-1):
    return jax.nn.softmax(x, axis=axis)

def _gelu(x):
    return jax.nn.gelu(x, approximate=True)

def _silu(x):
    return jax.nn.silu(x)

def _sigmoid(x):
    return jax.nn.sigmoid(x)

def _layernorm(x, axis=-1, eps=1e-05):
    m = jnp.mean(x, axis=axis, keepdims=True)
    v = jnp.var(x, axis=axis, keepdims=True)
    return (x - m) / jnp.sqrt(v + eps)

def _scatter_add(tgt, idx, src, axis=0):
    return tgt.at[idx].add(src)

def _segment_sum(src, seg, n):
    return jax.ops.segment_sum(src, seg, n)
kernel_name = 'mk_cond_resid_d2_seqx_r8_ab0e12'

def setup_inputs(seed: int=0):
    np.random.seed(seed)
    _w = jnp.asarray

    def _rec_inputs():
        import jax
        import jax.numpy as jnp
        _rk = jax.random.key(seed)
        x = -0.000125 + 0.9999 * jax.random.normal(jax.random.fold_in(_rk, 1), (64, 32, 128), jnp.float32)
        _lenS = 32 - jax.random.randint(jax.random.fold_in(_rk, 7), (64,), 0, max(1, 32 // 4) + 1, jnp.int32)
        _lenS2 = 32 - jax.random.randint(jax.random.fold_in(_rk, 8), (64,), 0, max(1, 32 // 4) + 1, jnp.int32)
        cond_1024 = 0.00513981 + 1.0024 * jax.random.normal(jax.random.fold_in(_rk, 11), (64, 128), jnp.float32)
        return (x, cond_1024)
    x, cond_1024 = _rec_inputs()

    def _L0_cond_setup():
        import jax, jax.numpy as jnp
        import numpy as np
        IN_FEATURES = 128
        OUT_FEATURES = 128
        BATCH = 32
        SEQ = 128
        EPS = 1e-08
        key = jax.random.key(seed)
        k1, k2, k3 = jax.random.split(key, 3)
        Efou = jax.random.normal(k1, (BATCH, SEQ, IN_FEATURES), dtype=jnp.float32)
        y = jax.random.normal(k2, (BATCH, IN_FEATURES), dtype=jnp.float32)
        weight = jax.random.normal(k3, (IN_FEATURES, OUT_FEATURES), dtype=jnp.float32)
        return {'Efou': Efou, 'y': y, 'weight': weight}
    _L0_cond_all = _L0_cond_setup()
    _L0_cond_in = {k: v for k, v in _L0_cond_all.items() if k in ('weight',)}
    del _L0_cond_all

    def _L1_cond_setup():
        import jax, jax.numpy as jnp
        import numpy as np
        D_MODEL = 128
        D_FF = 512
        N_EXPERTS = 8
        TOP_K = 2
        N_SHARED = 2
        B, T = (4, 256)
        key = jax.random.key(seed)
        ks = jax.random.split(key, 9)
        Hs = D_FF // 2
        Hr = D_FF // 4
        inp = {'x': jax.random.normal(ks[0], (B, T, D_MODEL), dtype=jnp.float32), 't_emb': jax.random.normal(ks[1], (B, D_MODEL), dtype=jnp.float32), 'W_router': 0.01 * jax.random.normal(ks[2], (N_EXPERTS, 2 * D_MODEL), dtype=jnp.float32), 'router_bias': jnp.zeros((N_EXPERTS,), dtype=jnp.float32), 's_w1': 0.02 * jax.random.normal(ks[3], (N_SHARED, Hs, D_MODEL), dtype=jnp.float32), 's_w3': 0.02 * jax.random.normal(ks[4], (N_SHARED, Hs, D_MODEL), dtype=jnp.float32), 's_w2': 0.02 * jax.random.normal(ks[5], (N_SHARED, D_MODEL, Hs), dtype=jnp.float32), 'r_w1': 0.02 * jax.random.normal(ks[6], (N_EXPERTS, Hr, D_MODEL), dtype=jnp.float32), 'r_w2': 0.02 * jax.random.normal(ks[7], (N_EXPERTS, D_MODEL, Hr), dtype=jnp.float32)}
        return inp
    _L1_cond_all = _L1_cond_setup()
    _L1_cond_in = {k: v for k, v in _L1_cond_all.items() if k in ('W_router', 'router_bias', 's_w1', 's_w3', 's_w2', 'r_w1', 'r_w2')}
    del _L1_cond_all
    return {'x': x, 'cond_1024': cond_1024, 'L0_cond_weight': _L0_cond_in['weight'], 'L1_cond_W_router': _L1_cond_in['W_router'], 'L1_cond_router_bias': _L1_cond_in['router_bias'], 'L1_cond_s_w1': _L1_cond_in['s_w1'], 'L1_cond_s_w3': _L1_cond_in['s_w3'], 'L1_cond_s_w2': _L1_cond_in['s_w2'], 'L1_cond_r_w1': _L1_cond_in['r_w1'], 'L1_cond_r_w2': _L1_cond_in['r_w2']}

def reference(x, cond_1024, L0_cond_weight, L1_cond_W_router, L1_cond_router_bias, L1_cond_s_w1, L1_cond_s_w3, L1_cond_s_w2, L1_cond_r_w1, L1_cond_r_w2):
    import jax
    import jax.numpy as jnp

    def _L0_cond_ref(Efou, y, weight):
        import jax, jax.numpy as jnp
        import numpy as np
        IN_FEATURES = 128
        OUT_FEATURES = 128
        BATCH = 32
        SEQ = 128
        EPS = 1e-08
        scale = 1.0 / np.sqrt(np.float32(weight.shape[0]))
        ys = y * scale
        d = jax.lax.rsqrt(jnp.einsum('bi,io->bo', ys * ys, weight * weight) + EPS)
        out = jnp.einsum('bsi,io->bso', Efou * ys[:, None, :], weight) * d[:, None, :]
        return out

    def _L1_cond_ref(x, t_emb, W_router, router_bias, s_w1, s_w3, s_w2, r_w1, r_w2):
        import jax, jax.numpy as jnp
        import numpy as np
        D_MODEL = 128
        D_FF = 512
        N_EXPERTS = 8
        TOP_K = 2
        N_SHARED = 2
        B, T = (4, 256)
        Bn, Tn, C = x.shape
        N = Bn * Tn
        x_flat = x.reshape(N, C)
        t_flat = jnp.broadcast_to(t_emb[:, None, :], (Bn, Tn, C)).reshape(N, C)
        shared_out = jnp.zeros_like(x_flat)
        for e in range(N_SHARED):
            h = jax.nn.silu(x_flat @ s_w1[e].T) * (x_flat @ s_w3[e].T)
            shared_out = shared_out + h @ s_w2[e].T
        shared_out = shared_out / N_SHARED
        router_in = jnp.concatenate([x_flat, t_flat], axis=-1)
        s = jax.nn.sigmoid((router_in @ W_router.T).astype(jnp.float32))
        sel_scores = s + router_bias
        _, topk_idx = jax.lax.top_k(sel_scores, TOP_K)
        s_sel = jnp.take_along_axis(s, topk_idx, axis=1)
        denom = jnp.sum(s_sel, axis=1, keepdims=True)
        gates = jnp.where(denom > 1e-09, s_sel / (denom + 1e-09), 1.0 / TOP_K).astype(x.dtype)
        gates_full = jnp.sum(jax.nn.one_hot(topk_idx, N_EXPERTS, dtype=x.dtype) * gates[..., None], axis=1)
        routed_out = jnp.zeros_like(x_flat)
        for e in range(N_EXPERTS):
            h = jax.nn.gelu(x_flat @ r_w1[e].T, approximate=False)
            routed_out = routed_out + h @ r_w2[e].T * gates_full[:, e:e + 1]
        out = (shared_out + routed_out) / (N_SHARED + TOP_K)
        return out.reshape(Bn, Tn, C)
    x = x + _L0_cond_ref(x, cond_1024, L0_cond_weight)
    x = x + _L1_cond_ref(x, cond_1024, L1_cond_W_router, L1_cond_router_bias, L1_cond_s_w1, L1_cond_s_w3, L1_cond_s_w2, L1_cond_r_w1, L1_cond_r_w2)
    return x

_drawn_inputs = setup_inputs


def setup_inputs(seed=0):
    import zlib

    import numpy as np

    out = dict(_drawn_inputs(seed))
    spreads = {'L1_cond_router_bias': (0.0, 0.8)}
    factors = {'L1_cond_W_router': 8.0,
     'L1_cond_s_w1': 8.0,
     'L1_cond_s_w3': 8.0,
     'L1_cond_s_w2': 8.0,
     'L1_cond_r_w1': 8.0,
     'L1_cond_r_w2': 8.0}
    for name, (base, spread) in spreads.items():
        noise = np.random.default_rng([zlib.crc32(name.encode()), seed]).standard_normal(out[name].shape)
        drawn = base * np.exp(spread * noise) if base else spread * noise
        out[name] = jnp.asarray(drawn.astype(out[name].dtype))
    for name, factor in factors.items():
        out[name] = (out[name] * factor).astype(out[name].dtype)
    return out
```

```python
from contextlib import ExitStack

import concourse.bass as bass
from concourse import mybir

F32 = mybir.dt.float32
F32R = mybir.dt.float32r
ALU = mybir.AluOpType
ACT = mybir.ActivationFunctionType
AX_X = mybir.AxisListType.X

C = 128
BATCH = 64
SEQ = 32
N = BATCH * SEQ
BLK = 512
NB = N // BLK
BPB = BLK // SEQ
TILES = N // 128
TPB = BLK // 128
BPT = 128 // SEQ
E = 8
CH = 4
NS = NB * CH
RING = 4
SKEW = 3
HALF = BLK // 2
EPS = 1e-8
XSCALE = float(C) ** -0.5
FAR = -3.0e38
GATE_OPS = 23


def low_on_pool(n):
    return n < NS and n % 2 == 0 and n > 0


POOL_LOWS = sum(low_on_pool(n) for n in range(NS))


def build(nc, xT, condT, w0, w_up, w_down, small_rows, outT):
    with ExitStack() as ctx:
        def sb(name, shape, dt=F32):
            return ctx.enter_context(nc.sbuf_tensor(name, shape, dt))

        def sem(name):
            return ctx.enter_context(nc.semaphore(name))

        x = sb("x", [C, N])
        cond = sb("cond", [C, BATCH])
        mod_w = sb("mod_w", [C, C])
        up_w = sb("up_w", [C, (2 * CH + E) * C])
        up_hi = sb("up_hi", [C, (2 * CH + E) * C], F32R)
        up_lo = sb("up_lo", [C, (2 * CH + E) * C], F32R)
        down_w = sb("down_w", [C, (CH + E) * C])
        down_hi = sb("down_hi", [C, (CH + E) * C], F32R)
        down_lo = sb("down_lo", [C, (CH + E) * C], F32R)
        small = sb("small", [128, 4 * E + 256])
        router_w = small[:, 0:2 * E]
        bias = small[:, 2 * E:3 * E]
        order = small[:, 3 * E:4 * E]
        eye = small[:, 4 * E:4 * E + 128]
        own_batch = small[0:BPT, 4 * E + 128:]
        router_hi = sb("router_hi", [C, 128], F32R)
        router_lo = sb("router_lo", [C, 128], F32R)

        ys = sb("ys", [C, BATCH])
        ys_sq = sb("ys_sq", [C, BATCH])
        mod_sq = sb("mod_sq", [C, C])
        demod_var = sb("demod_var", [C, BATCH])
        demod_inv = sb("demod_inv", [C, BATCH])
        demod = sb("demod", [C, BATCH])
        xy = sb("xy", [C, N])
        scaled = sb("scaled", [C, N])
        x1 = sb("x1", [C, N])
        x1_hi = sb("x1_hi", [C, N], F32R)
        x1_lo = sb("x1_lo", [C, N], F32R)

        batch_logit = sb("batch_logit", [BPT, TILES, E])
        cond_logit = sb("cond_logit", [128, TILES, E])
        logit = sb("logit", [E, N])
        full_logit = sb("full_logit", [128, TILES, E])
        score = sb("score", [128, TILES, E])
        biased = sb("biased", [128, TILES, E])
        rest = sb("rest", [128, TILES, E])
        best = sb("best", [128, 2, TILES])
        is_best = sb("is_best", [128, 2, TILES, E])
        ranked = sb("ranked", [128, 2, TILES, E])
        rank = sb("rank", [128, 2, TILES])
        pick = sb("pick", [128, 2, TILES, E])
        picked = sb("picked", [128, TILES, E])
        kept = sb("kept", [128, TILES, E])
        denom = sb("denom", [128, TILES])
        usable = sb("usable", [128, TILES])
        denom_eps = sb("denom_eps", [128, TILES])
        recip = sb("recip", [128, TILES])
        by_score = sb("by_score", [128, TILES])
        by_half = sb("by_half", [128, TILES])
        gate_a = sb("gate_a", [128, TILES, E])
        gate_b = sb("gate_b", [128, TILES, E])
        gate = sb("gate", [128, TILES, E])
        gate_rows = sb("gate_rows", [E, N])
        gate_line = sb("gate_line", [1, 2, E, BLK])
        gate_wide = sb("gate_wide", [128, RING, BLK])

        activated = sb("activated", [C, RING, BLK])
        hidden = sb("hidden", [C, RING, BLK])
        hid_hi = sb("hid_hi", [C, RING, BLK], F32R)
        hid_lo = sb("hid_lo", [C, RING, BLK], F32R)
        partial = scaled
        result = xy

        up_ps = ctx.enter_context(nc.psum_tensor("up_ps", [128, 4, BLK], F32))
        acc_ps = ctx.enter_context(nc.psum_tensor("acc_ps", [128, 2, BLK], F32))
        misc_ps = ctx.enter_context(nc.psum_tensor("misc_ps", [128, 2, BLK], F32))
        mod_half_ps = [acc_ps[:, 0, 0:HALF], up_ps[:, 0, 0:HALF]]
        mod_ps = [None, acc_ps[:, 1, :], misc_ps[:, 0, :], misc_ps[:, 1, :]]
        demod_ps = up_ps[:, 2, 0:BATCH]
        batch_logit_ps = up_ps[0:BPT, 3, 0:TILES * E].rearrange("p (t e) -> p t e", e=E)
        cond_logit_ps = up_ps[:, 3, TILES * E:2 * TILES * E].rearrange("p (t e) -> p t e", e=E)
        logit_ps = misc_ps[:, 0, 0:TILES * E].rearrange("p (t e) -> p t e", e=E)

        in_cond, in_mod_w, in_small = sem("in_cond"), sem("in_mod_w"), sem("in_small")
        in_x0b = sem("in_x0b")
        in_x = [sem(f"in_x{b}") for b in range(NB)]
        in_up_s = [sem(f"in_up_s{h}") for h in range(2)]
        in_up_r, in_down_s, in_down_r = sem("in_up_r"), sem("in_down_s"), sem("in_down_r")
        up_hi_dve = sem("up_hi_dve")
        up_hi_s, up_lo_s, down_hi_s, down_lo_s = sem("up_hi_s"), sem("up_lo_s"), sem("down_hi_s"), sem("down_lo_s")
        routed_hi, routed_lo = sem("routed_hi"), sem("routed_lo")
        router_zero, router_hi_done, router_split = sem("router_zero"), sem("router_hi_done"), sem("router_split")
        mod_sq_done = sem("mod_sq_done")
        ys_ready, squares_ready, demod_mm, demod_var_done = sem("ys_ready"), sem("squares_ready"), sem("demod_mm"), sem("demod_var_done")
        demod_inv_done, demod_ready = sem("demod_inv_done"), sem("demod_ready")
        xy_dve, xy_pool = sem("xy_dve"), sem("xy_pool")
        mod_mm, scaled_done, x1_done, x1_hi_done, x1_lo_dve, x1_lo_pool = (
            sem("mod_mm"), sem("scaled_done"), sem("x1_done"), sem("x1_hi_done"), sem("x1_lo_dve"), sem("x1_lo_pool"))
        batch_logit_mm, batch_logit_done = sem("batch_logit_mm"), sem("batch_logit_done")
        cond_logit_mm, cond_logit_done, logit_mm, logit_done, full_logit_done = (
            sem("cond_logit_mm"), sem("cond_logit_done"), sem("logit_mm"), sem("logit_done"), sem("full_logit_done"))
        logit_turned, score_done, router_chain = sem("logit_turned"), sem("score_done"), sem("router_chain")
        gate_turned, gate_rows_done, gate_wide_done = sem("gate_turned"), sem("gate_rows_done"), sem("gate_wide_done")
        gate_lined = sem("gate_lined")
        pre_ready, mul_ready, act_done, hidden_done = sem("pre_ready"), sem("mul_ready"), sem("act_done"), sem("hidden_done")
        hi_done, lo_dve, lo_pool, down_done = sem("hi_done"), sem("lo_dve"), sem("lo_pool"), sem("down_done")
        acc_taken, out_done = sem("acc_taken"), sem("out_done")

        SH = 2 * CH * C
        SD = CH * C

        routed_pieces = [(up_w, up_hi, SH + c * BLK) for c in range(E * C // BLK)]
        routed_pieces += [(down_w, down_hi, SD + c * BLK) for c in range(E * C // BLK)]

        def tok(b):
            return bass.ds(b * BLK, BLK)

        def by_batch(ap):
            return ap.rearrange("p (b s) -> p b s", s=SEQ)

        block = ctx.enter_context(nc.Block())

        def half(h):
            return bass.ds(h * HALF, HALF)

        def batches(t, at, n):
            return t[:, at:at + n].unsqueeze(2).broadcast_to([t.shape[0], n, SEQ])


        @block.sync
        def _(sp):
            sp.dma_start(cond[:], condT).then_inc(in_cond, 16)
            sp.dma_start(x[:, half(0)], xT[:, half(0)]).then_inc(in_x[0], 16)
            sp.dma_start(x[:, half(1)], xT[:, half(1)]).then_inc(in_x0b, 16)
            sp.dma_start(up_w[:, 0:SH // 2], w_up[:, 0:SH // 2]).then_inc(in_up_s[0], 16)
            for b in range(1, NB):
                sp.dma_start(x[:, tok(b)], xT[:, tok(b)]).then_inc(in_x[b], 16)
            sp.dma_start(up_w[:, SH:], w_up[:, SH:]).then_inc(in_up_r, 16)
            sp.dma_start(down_w[:, SD:], w_down[:, SD:]).then_inc(in_down_r, 16)
            for b in range(NB):
                sp.wait_ge(gate_rows_done, b + 1)
                if b >= 1:
                    sp.wait_ge(gate_lined, 16 * b)
                if b >= 2:
                    sp.wait_ge(gate_wide_done, E * (b - 1))
                sp.dma_start(gate_line[0:1, b % 2], gate_rows[:, tok(b)]).then_inc(gate_lined, 16)
            for b in range(NB):
                sp.wait_ge(acc_taken, NB + b + 1)
                sp.dma_start(outT[:, tok(b)], result[:, tok(b)]).then_inc(out_done, 16)
            sp.wait_ge(out_done, 16 * NB)

        @block.scalar
        def _(act):
            act.dma_start(small[:], small_rows).then_inc(in_small, 16)
            act.dma_start(mod_w[:], w0).then_inc(in_mod_w, 16)
            act.dma_start(up_w[:, SH // 2:SH], w_up[:, SH // 2:SH]).then_inc(in_up_s[1], 16)
            act.dma_start(down_w[:, 0:SD], w_down[:, 0:SD]).then_inc(in_down_s, 16)

            def copy(out, in_):
                return nc.scalar.activation(out, in_, ACT.Copy)

            act.wait_ge(demod_inv_done, 1)
            nc.scalar.activation(demod[:], demod_inv[:], ACT.Sqrt).then_inc(demod_ready, 1)
            act.wait_ge(in_up_s[1], 16)
            copy(up_hi[:, SH // 2:SH], up_w[:, SH // 2:SH]).then_inc(up_hi_s, 1)
            for h in range(2):
                act.wait_ge(x1_done, h + 1)
                copy(x1_hi[:, half(h)], x1[:, half(h)]).then_inc(x1_hi_done, 1)
            act.wait_ge(in_down_s, 16)
            copy(down_hi[:, 0:SD], down_w[:, 0:SD]).then_inc(down_hi_s, 1)

            def high(buf, n):
                act.wait_ge(hidden_done, n + 1)
                copy(hid_hi[:, buf, :], hidden[:, buf, :]).then_inc(hi_done, 1)

            for n in range(NS):
                act.wait_ge(pre_ready, n + 1)
                nc.scalar.activation(activated[:, n % RING, :], up_ps[:, 2 * (n % 2), :], ACT.Silu).then_inc(act_done, 1)
                if n in (0, 1, 2):
                    b = n + 1
                    act.wait_ge(x1_done, b + 2)
                    copy(x1_hi[:, tok(b)], x1[:, tok(b)]).then_inc(x1_hi_done, 1)
                if n >= 1:
                    high((n - 1) % RING, n - 1)
                for b in {3: (0, 1), 4: (2,), 5: (3,)}.get(n, ()):
                    act.wait_ge(logit_mm, b + 1)
                    copy(logit[:, tok(b)], misc_ps[0:E, b % 2, :]).then_inc(logit_done, 1)
                if n == 7:
                    act.wait_ge(full_logit_done, 1)
                    nc.scalar.activation(score[:], full_logit[:], ACT.Sigmoid).then_inc(score_done, 1)
                if 8 <= n < 12:
                    full, upper, at = routed_pieces[n - 8]
                    if n == 8:
                        act.wait_ge(in_up_r, 16)
                        act.wait_ge(in_down_r, 16)
                    copy(upper[:, bass.ds(at, BLK)], full[:, bass.ds(at, BLK)]).then_inc(routed_hi, 1)
                if n >= NS - 2:
                    for b in (2 * (n - NS + 2), 2 * (n - NS + 2) + 1):
                        act.wait_ge(gate_turned, b + 1)
                        copy(gate_rows[:, tok(b)], misc_ps[0:E, b % 2, :]).then_inc(gate_rows_done, 1)

            with act.Fori(0, NB) as b:
                for e in range(E):
                    n = NS + E * b + e
                    act.wait_ge(pre_ready, n + 1)
                    nc.scalar.activation(activated[:, e % RING, :], up_ps[:, e % 4, :], ACT.Gelu).then_inc(act_done, 1)
                    high((e - 1) % RING, n - 1)
            high((E - 1) % RING, NS + NB * E - 1)

        @block.vector
        def _(dve):
            def mult(out, a, b):
                return nc.vector.tensor_tensor(out, a, b, ALU.mult)

            def sub(out, a, b):
                return nc.vector.tensor_tensor(out, a, b, ALU.subtract)

            dve.wait_ge(in_cond, 16)
            nc.vector.tensor_scalar(ys[:], cond[:], XSCALE, None, ALU.mult).then_inc(ys_ready, 1)
            dve.wait_ge(ys_ready, 1)
            mult(ys_sq[:], ys[:], ys[:]).then_inc(squares_ready, 1)
            for h in range(2):
                dve.wait_ge(in_x0b if h else in_x[0], 16)
                mult(by_batch(xy[:, half(h)]), by_batch(x[:, half(h)]),
                     batches(ys, h * BPB // 2, BPB // 2)).then_inc(xy_dve, 1)
            dve.wait_ge(batch_logit_mm, 1)
            nc.vector.tensor_copy(batch_logit[:], batch_logit_ps).then_inc(batch_logit_done, 1)
            dve.wait_ge(in_up_s[0], 16)
            nc.vector.tensor_copy(up_hi[:, 0:SH // 2], up_w[:, 0:SH // 2]).then_inc(up_hi_dve, 1)
            dve.wait_ge(demod_mm, 1)
            nc.vector.tensor_scalar(demod_var[:], demod_ps, EPS, None, ALU.add).then_inc(demod_var_done, 1)
            dve.wait_ge(demod_var_done, 1)
            nc.vector.reciprocal(demod_inv[:], demod_var[:]).then_inc(demod_inv_done, 1)
            dve.wait_ge(in_x[1], 16)
            mult(by_batch(xy[:, tok(1)]), by_batch(x[:, tok(1)]), batches(ys, BPB, BPB)).then_inc(xy_dve, 1)
            dve.wait_ge(demod_ready, 1)

            def residual(part, mod, first_batch, count):
                dve.wait_ge(mod_mm, count)
                mult(by_batch(scaled[:, part]), by_batch(mod),
                     batches(demod, first_batch, mod.shape[1] // SEQ)).then_inc(scaled_done, 1)
                dve.wait_ge(scaled_done, count)
                nc.vector.tensor_tensor(x1[:, part], scaled[:, part], x[:, part], ALU.add).then_inc(x1_done, 1)

            for h in range(2):
                residual(half(h), mod_half_ps[h], h * BPB // 2, h + 1)
            for h in range(2):
                dve.wait_ge(x1_hi_done, h + 1)
                sub(x1_lo[:, half(h)], x1[:, half(h)], x1_hi[:, half(h)]).then_inc(x1_lo_dve, 1)
            dve.wait_ge(cond_logit_mm, 1)
            nc.vector.tensor_copy(cond_logit[:], cond_logit_ps).then_inc(cond_logit_done, 1)

            def wide(ap):
                return ap.unsqueeze(2).broadcast_to([128, TILES, E])

            def rows(ap):
                return ap.unsqueeze(1).broadcast_to([128, TILES, E])

            def pick_best(k, values):
                yield nc.vector.tensor_reduce(best[:, k, :], values[:], AX_X, ALU.max)
                yield nc.vector.tensor_tensor(is_best[:, k], values[:], wide(best[:, k, :]), ALU.is_equal)
                yield mult(ranked[:, k], is_best[:, k], rows(order))
                yield nc.vector.tensor_reduce(rank[:, k, :], ranked[:, k], AX_X, ALU.max)
                yield nc.vector.tensor_tensor(pick[:, k], rows(order), wide(rank[:, k, :]), ALU.is_equal)

            def gate_operations():
                yield nc.vector.tensor_tensor(biased[:], score[:], rows(bias), ALU.add)
                yield from pick_best(0, biased)
                yield nc.vector.scalar_tensor_tensor(rest[:], pick[:, 0], FAR, biased[:], ALU.mult, ALU.add)
                yield from pick_best(1, rest)
                yield nc.vector.tensor_tensor(picked[:], pick[:, 0], pick[:, 1], ALU.add)
                yield mult(kept[:], score[:], picked[:])
                yield nc.vector.tensor_reduce(denom[:], kept[:], AX_X, ALU.add)
                yield nc.vector.tensor_scalar(usable[:], denom[:], 1e-9, None, ALU.is_gt)
                yield nc.vector.tensor_scalar(denom_eps[:], denom[:], 1e-9, None, ALU.add)
                yield nc.vector.reciprocal(recip[:], denom_eps[:])
                yield mult(by_score[:], recip[:], usable[:])
                yield nc.vector.tensor_scalar(by_half[:], usable[:], -0.5, 0.5, ALU.mult, ALU.add)
                yield mult(gate_a[:], kept[:], wide(by_score[:]))
                yield mult(gate_b[:], picked[:], wide(by_half[:]))
                yield nc.vector.tensor_tensor(gate[:], gate_a[:], gate_b[:], ALU.add)

            gates = gate_operations()
            made = [0]

            def gate_step(times=1):
                for _ in range(times):
                    if made[0] < GATE_OPS:
                        if made[0]:
                            dve.wait_ge(router_chain, made[0])
                        next(gates).then_inc(router_chain, 1)
                        made[0] += 1

            def take_shared(b):
                dve.wait_ge(down_done, CH * (b + 1))
                nc.vector.scalar_tensor_tensor(partial[:, tok(b)], acc_ps[:, b % 2, :], 0.125, x1[:, tok(b)],
                                               ALU.mult, ALU.add).then_inc(acc_taken, 1)

            def low(buf, n):
                dve.wait_ge(hi_done, n + 1)
                sub(hid_lo[:, buf, :], hidden[:, buf, :], hid_hi[:, buf, :]).then_inc(lo_dve, 1)

            for n in range(NS):
                in_gates = n >= 7
                if n == 7:
                    dve.wait_ge(score_done, 1)
                if in_gates:
                    gate_step()
                dve.wait_ge(act_done, n + 1)
                dve.wait_ge(mul_ready, n + 1)
                mult(hidden[:, n % RING, :], activated[:, n % RING, :], up_ps[:, 2 * (n % 2) + 1, :]).then_inc(hidden_done, 1)
                if n + 1 < NB:
                    residual(tok(n + 1), mod_ps[n + 1], (n + 1) * BPB, n + 3)
                if in_gates:
                    gate_step()
                if n >= 1 and not low_on_pool(n - 1):
                    low((n - 1) % RING, n - 1)
                elif in_gates:
                    gate_step(2)
                if n == 6:
                    dve.wait_ge(logit_turned, 1)
                    dve.wait_ge(cond_logit_done, 1)
                    nc.vector.tensor_tensor(full_logit[:], logit_ps, cond_logit[:], ALU.add).then_inc(full_logit_done, 1)
                if in_gates:
                    gate_step()
                if n % CH == SKEW and n > CH:
                    take_shared(n // CH - 1)
            gate_step(GATE_OPS)

            def routed_step(b, e):
                n = NS + E * b + e
                dve.wait_ge(gate_wide_done, E * b + e + 1)
                dve.wait_ge(act_done, n + 1)
                mult(hidden[:, e % RING, :], activated[:, e % RING, :], gate_wide[:, e % RING, :]).then_inc(hidden_done, 1)
                low((e - 1) % RING, n - 1)

            def take_routed(b):
                dve.wait_ge(down_done, NS + E * (b + 1))
                nc.vector.scalar_tensor_tensor(result[:, tok(b)], acc_ps[:, b % 2, :], 0.25, partial[:, tok(b)],
                                               ALU.mult, ALU.add).then_inc(acc_taken, 1)

            for e in range(E):
                routed_step(0, e)
                if e == SKEW:
                    take_shared(NB - 1)
            with dve.Fori(1, NB) as b:
                for e in range(E):
                    routed_step(b, e)
                    if e == SKEW:
                        take_routed(b - 1)
            low((E - 1) % RING, NS + NB * E - 1)
            take_routed(NB - 1)

        @block.gpsimd
        def _(pool):
            def sub(out, full, upper):
                return nc.gpsimd.tensor_tensor(out, full, upper, ALU.subtract)

            nc.gpsimd.memset(router_hi[:].bitcast(F32), 0.0)
            nc.gpsimd.memset(router_lo[:].bitcast(F32), 0.0).then_inc(router_zero, 1)
            pool.wait_ge(in_mod_w, 16)
            nc.gpsimd.tensor_tensor(mod_sq[:], mod_w[:], mod_w[:], ALU.mult).then_inc(mod_sq_done, 1)

            def up_low(c):
                part = bass.ds(c * 2 * C, 2 * C)
                sub(up_lo[:, part], up_w[:, part], up_hi[:, part]).then_inc(up_lo_s, 1)

            def modulate(b):
                pool.wait_ge(in_x[b], 16)
                nc.gpsimd.tensor_tensor(by_batch(xy[:, tok(b)]), by_batch(x[:, tok(b)]), batches(ys, b * BPB, BPB),
                                        ALU.mult).then_inc(xy_pool, 1)

            pool.wait_ge(up_hi_dve, 1)
            up_low(0)
            up_low(1)
            pool.wait_ge(ys_ready, 1)
            modulate(2)
            modulate(3)
            pool.wait_ge(up_hi_s, 1)
            up_low(2)
            pool.wait_ge(down_hi_s, 1)
            sub(down_lo[:, 0:SD], down_w[:, 0:SD], down_hi[:, 0:SD]).then_inc(down_lo_s, 1)
            up_low(3)
            pool.wait_ge(in_small, 16)
            pool.wait_ge(router_zero, 1)
            nc.gpsimd.tensor_copy(router_hi[:, 0:E], router_w[:, 0:E]).then_inc(router_hi_done, 1)
            for b in range(1, NB):
                pool.wait_ge(x1_hi_done, b + 2)
                sub(x1_lo[:, tok(b)], x1[:, tok(b)], x1_hi[:, tok(b)]).then_inc(x1_lo_pool, 1)
                if b == 1:
                    pool.wait_ge(router_hi_done, 1)
                    sub(router_lo[:, 0:E], router_w[:, 0:E], router_hi[:, 0:E]).then_inc(router_split, 1)
            piece = 0
            for n in range(NS):
                if low_on_pool(n):
                    pool.wait_ge(hi_done, n + 1)
                    sub(hid_lo[:, n % RING, :], hidden[:, n % RING, :], hid_hi[:, n % RING, :]).then_inc(lo_pool, 1)
                    if n >= 8 and piece < len(routed_pieces):
                        for _ in range(1 if n < NS - 2 else 4):
                            if piece < len(routed_pieces):
                                full, upper, at = routed_pieces[piece]
                                lower = up_lo if full is up_w else down_lo
                                part = bass.ds(at, BLK)
                                pool.wait_ge(routed_hi, piece + 1)
                                sub(lower[:, part], full[:, part], upper[:, part]).then_inc(routed_lo, 1)
                                piece += 1
            for m in range(NB * E):
                b, e = divmod(m, E)
                if e == 0:
                    pool.wait_ge(gate_lined, 16 * (b + 1))
                if m >= RING:
                    pool.wait_ge(hidden_done, NS + m - RING + 1)
                nc.gpsimd.partition_broadcast(gate_wide[:, m % RING, :], gate_line[0:1, b % 2, e, :]).then_inc(gate_wide_done, 1)

        @block.tensor
        def _(pe):
            def three_passes(out, w_hi, w_lo, v_hi, v_lo, first=True, last=True):
                nc.tensor.matmul(out, w_hi, v_hi, start=first, stop=False)
                nc.tensor.matmul(out, w_hi, v_lo, start=False, stop=False)
                return nc.tensor.matmul(out, w_lo, v_hi, start=False, stop=last)


            def modulated(b):
                nc.tensor.matmul(mod_ps[b], mod_w[:], xy[:, tok(b)], start=True, stop=True).then_inc(mod_mm, 1)

            pe.wait_ge(in_small, 16)
            pe.wait_ge(in_cond, 16)
            for t in range(TILES):
                last = nc.tensor.matmul(batch_logit_ps[:, t, :], cond[:, bass.ts(t, BPT)], router_w[:, E:2 * E],
                                        start=True, stop=True)
            last.then_inc(batch_logit_mm, 1)
            pe.wait_ge(in_mod_w, 16)
            pe.wait_ge(xy_dve, 1)
            nc.tensor.matmul(mod_half_ps[0], mod_w[:], xy[:, half(0)], start=True, stop=True).then_inc(mod_mm, 1)
            pe.wait_ge(squares_ready, 1)
            pe.wait_ge(mod_sq_done, 1)
            nc.tensor.matmul(demod_ps, mod_sq[:], ys_sq[:], start=True, stop=True).then_inc(demod_mm, 1)
            pe.wait_ge(xy_dve, 2)
            nc.tensor.matmul(mod_half_ps[1], mod_w[:], xy[:, half(1)], start=True, stop=True).then_inc(mod_mm, 1)
            pe.wait_ge(batch_logit_done, 1)
            nc.tensor.matmul(cond_logit_ps, own_batch, batch_logit[:], start=True, stop=True).then_inc(cond_logit_mm, 1)
            pe.wait_ge(xy_dve, 3)
            modulated(1)

            def shared_up(n):
                b, j = divmod(n, CH)
                parts = [tok(b)]
                if n == 0:
                    parts = [half(0), half(1)]
                elif j == 0:
                    pe.wait_ge(x1_hi_done, b + 2)
                    pe.wait_ge(x1_lo_pool, b)
                if b == 0:
                    pe.wait_ge(up_lo_s, j + 1)
                if n >= 2:
                    pe.wait_ge(act_done, n - 1)
                if n == 1:
                    pe.wait_ge(demod_var_done, 1)
                    pe.wait_ge(cond_logit_done, 1)
                for k, (ready, weights) in enumerate(((pre_ready, bass.ds(2 * j * C, C)), (mul_ready, bass.ds((2 * j + 1) * C, C)))):
                    if k == 1 and n >= 2:
                        pe.wait_ge(hidden_done, n - 1)
                    for h, part in enumerate(parts):
                        if n == 0 and k == 0:
                            pe.wait_ge(x1_lo_dve, h + 1)
                        out = up_ps[:, 2 * (n % 2) + k, half(h) if n == 0 else slice(0, BLK)]
                        last = three_passes(out, up_hi[:, weights], up_lo[:, weights], x1_hi[:, part], x1_lo[:, part])
                    last.then_inc(ready, 1)

            def down(out, weights, n, buf, first, last):
                pe.wait_ge(hi_done, n + 1)
                if isinstance(n, int) and low_on_pool(n):
                    pe.wait_ge(lo_pool, sum(low_on_pool(i) for i in range(n + 1)))
                elif isinstance(n, int) and n < NS:
                    pe.wait_ge(lo_dve, sum(not low_on_pool(i) for i in range(n + 1)))
                else:
                    pe.wait_ge(lo_dve, n + 1 - POOL_LOWS)
                three_passes(out, down_hi[:, weights], down_lo[:, weights],
                             hid_hi[:, buf, :], hid_lo[:, buf, :], first=first, last=last).then_inc(down_done, 1)

            def shared_down(n):
                b, j = divmod(n, CH)
                if n == 0:
                    pe.wait_ge(down_lo_s, 1)
                if j == 0:
                    if b < 2:
                        pe.wait_ge(scaled_done, b + 2)
                    else:
                        pe.wait_ge(acc_taken, b - 1)
                down(acc_ps[:, b % 2, :], bass.ts(j, C), n, n % RING, j == 0, j == CH - 1)

            def logits(b):
                if b > 0:
                    pe.wait_ge(x1_lo_pool, b)
                pe.wait_ge(router_split, 1)
                if b < 2:
                    pe.wait_ge(scaled_done, b + 4)
                else:
                    pe.wait_ge(logit_done, b - 1)
                three_passes(misc_ps[:, b % 2, :], router_hi[:], router_lo[:],
                             x1_hi[:, tok(b)], x1_lo[:, tok(b)]).then_inc(logit_mm, 1)

            def turn_gates(b):
                if b == 0:
                    pe.wait_ge(router_chain, GATE_OPS)
                if b >= 2:
                    pe.wait_ge(gate_rows_done, b - 1)
                for t in range(TPB):
                    last = nc.tensor.transpose(misc_ps[0:E, b % 2, bass.ts(t, 128)], gate[:, b * TPB + t, :], eye)
                last.then_inc(gate_turned, 1)

            for n in range(NS):
                shared_up(n)
                if n < 2:
                    pe.wait_ge(xy_pool, n + 1)
                    modulated(n + 2)
                if n >= SKEW:
                    shared_down(n - SKEW)
                for b in {3: (0, 1), 4: (2,), 5: (3,)}.get(n, ()):
                    logits(b)
                if n == 6:
                    pe.wait_ge(logit_done, NB)
                    for t in range(TILES):
                        last = nc.tensor.transpose(logit_ps[:, t, :], logit[:, bass.ts(t, 128)], eye[0:E, 0:E])
                    last.then_inc(logit_turned, 1)
                if n >= NS - 2:
                    turn_gates(2 * (n - NS + 2))
                    turn_gates(2 * (n - NS + 2) + 1)

            def routed_up(b, e):
                w1 = bass.ds(SH + e * C, C)
                if isinstance(b, int) and e < 4:
                    pe.wait_ge(hidden_done, NS - 1 if e < 2 else NS)
                three_passes(up_ps[:, e % 4, :], up_hi[:, w1], up_lo[:, w1],
                             x1_hi[:, tok(b)], x1_lo[:, tok(b)]).then_inc(pre_ready, 1)

            def routed_down(b, e):
                if e == 0:
                    pe.wait_ge(acc_taken, NB + b - 1)
                down(acc_ps[:, b % 2, :], bass.ds(SD + e * C, C), NS + E * b + e, e % RING, e == 0, e == E - 1)

            pe.wait_ge(routed_lo, len(routed_pieces))
            for e in range(E):
                routed_up(0, e)
                if e < SKEW:
                    shared_down(NS - SKEW + e)
                else:
                    routed_down(0, e - SKEW)
            with pe.Fori(1, NB) as b:
                for e in range(E):
                    routed_up(b, e)
                    if e < SKEW:
                        routed_down(b - 1, E + e - SKEW)
                    else:
                        routed_down(b, e - SKEW)
            for e in range(E - SKEW, E):
                routed_down(NB - 1, e)


def kernel(**inputs):
    import numpy as np
    import concourse.bacc as bacc
    from concourse.bass_utils import run_bass_kernel_spmd

    a = {k: np.asarray(v) for k, v in inputs.items()}
    s_w1, s_w3 = (a[f"L1_cond_{k}"].reshape(CH, C, C) for k in ("s_w1", "s_w3"))
    s_w2 = a["L1_cond_s_w2"].reshape(2, C, 2, C).transpose(0, 2, 3, 1).reshape(CH * C, C)
    shared_up = np.stack([s_w1, s_w3], axis=1).reshape(2 * CH * C, C)
    routed_up = a["L1_cond_r_w1"].reshape(E * C, C)
    routed_down = a["L1_cond_r_w2"].transpose(0, 2, 1).reshape(E * C, C)
    down = np.concatenate([s_w2, routed_down]).reshape(CH + E, C, C).transpose(1, 0, 2)
    router = a["L1_cond_W_router"]
    arrays = {
        "xT": a["x"].reshape(N, C).T,
        "condT": a["cond_1024"].T,
        "w0": a["L0_cond_weight"],
        "w_up": np.concatenate([shared_up, routed_up]).T,
        "w_down": down.reshape(C, (CH + E) * C),
        "small_rows": np.concatenate([
            router[:, :C].T, router[:, C:].T,
            np.broadcast_to(a["L1_cond_router_bias"], (128, E)),
            np.broadcast_to(np.arange(E, 0, -1, dtype=np.float32), (128, E)),
            np.eye(128, dtype=np.float32),
            np.tile(np.repeat(np.eye(BPT, dtype=np.float32), SEQ, axis=1), (128 // BPT, 1))], axis=1),
    }
    arrays = {k: np.ascontiguousarray(v) for k, v in arrays.items()}
    nc = bacc.Bacc("TRN2", target_bir_lowering=False, num_devices=1)
    args = [nc.dram_tensor(k, v.shape, mybir.dt.from_np(v.dtype), kind="ExternalInput").ap() for k, v in arrays.items()]
    out = nc.dram_tensor("outT", (C, N), F32, kind="ExternalOutput").ap()
    build(nc, *args, out)
    r = run_bass_kernel_spmd(nc, [arrays], core_ids=[0])
    return r.results[0]["outT"].T.reshape(BATCH, SEQ, C)
```

```python
from contextlib import ExitStack

import concourse.bass as bass
from concourse import mybir

F32 = mybir.dt.float32
F32R = mybir.dt.float32r
ALU = mybir.AluOpType
ACT = mybir.ActivationFunctionType
AX_X = mybir.AxisListType.X

C = 128
BATCH = 64
SEQ = 32
N = BATCH * SEQ
BLK = 512
NB = N // BLK
BPB = BLK // SEQ
TILES = N // 128
TPB = BLK // 128
BPT = 128 // SEQ
E = 8
CH = 4
NS = NB * CH
RING = 8
ARING = 4
GRING = 4
SKEW = 5
HALF = BLK // 2
EPS = 1e-8
XSCALE = float(C) ** -0.5
FAR = -3.0e38
WARM_BEFORE = 7
WARM_AFTER = 5
GATE_OPS = 23
LOGITS_AFTER = {3: (0,), 4: (1,), 5: (2, 3)}
TURN_AFTER = 6
SPLIT_AFTER = [5, 8, 9, 11]
LOWS_AFTER = [6, 8, 10, 12]


POOL_EXPERTS = (2, 5)


def low_on_pool(n):
    return n % 2 == 0 and n >= 4


def pool_experts(e):
    return sum(i <= e for i in POOL_EXPERTS)


LOW_AFTER = {3: (0, 1), 4: (2,), 5: (3,)} | {n + 1: (n,) for n in range(NB, NS - 1) if not low_on_pool(n)}
POOL_LOWS = sum(low_on_pool(n) for n in range(NS))


def build(nc, xT, condT, w0, w_up, w_down, small_rows, outT):
    with ExitStack() as ctx:
        def sb(name, shape, dt=F32):
            return ctx.enter_context(nc.sbuf_tensor(name, shape, dt))

        def sem(name):
            return ctx.enter_context(nc.semaphore(name))

        x = sb("x", [C, N])
        cond = sb("cond", [C, BATCH])
        mod_w = sb("mod_w", [C, C])
        up_w = sb("up_w", [C, (2 * CH + E) * C])
        up_hi = sb("up_hi", [C, (2 * CH + E) * C], F32R)
        up_lo = sb("up_lo", [C, (2 * CH + E) * C], F32R)
        down_w = sb("down_w", [C, (CH + E) * C])
        down_hi = sb("down_hi", [C, (CH + E) * C], F32R)
        down_lo = sb("down_lo", [C, (CH + E) * C], F32R)
        small = sb("small", [128, 4 * E + 256])
        router_w = small[:, 0:2 * E]
        bias = small[:, 2 * E:3 * E]
        order = small[:, 3 * E:4 * E]
        eye = small[:, 4 * E:4 * E + 128]
        own_batch = small[0:BPT, 4 * E + 128:]
        router_hi = sb("router_hi", [C, 128], F32R)
        router_lo = sb("router_lo", [C, 128], F32R)

        ys = sb("ys", [C, BATCH])
        ys_sq = sb("ys_sq", [C, BATCH])
        mod_sq = sb("mod_sq", [C, C])
        demod_var = sb("demod_var", [C, BATCH])
        demod_inv = sb("demod_inv", [C, BATCH])
        demod = sb("demod", [C, BATCH])
        xy = sb("xy", [C, N])
        scaled = sb("scaled", [C, N])
        x1 = sb("x1", [C, N])
        x1_hi = sb("x1_hi", [C, N], F32R)
        x1_lo = sb("x1_lo", [C, N], F32R)

        batch_logit = sb("batch_logit", [BPT, TILES, E])
        cond_logit = sb("cond_logit", [128, TILES, E])
        full_logit = sb("full_logit", [128, TILES, E])
        score = sb("score", [128, TILES, E])
        biased = sb("biased", [128, TILES, E])
        rest = sb("rest", [128, TILES, E])
        best = sb("best", [128, 2, TILES])
        is_best = sb("is_best", [128, 2, TILES, E])
        ranked = sb("ranked", [128, 2, TILES, E])
        rank = sb("rank", [128, 2, TILES])
        pick = sb("pick", [128, 2, TILES, E])
        picked = sb("picked", [128, TILES, E])
        kept = sb("kept", [128, TILES, E])
        denom = sb("denom", [128, TILES])
        usable = sb("usable", [128, TILES])
        denom_eps = sb("denom_eps", [128, TILES])
        recip = sb("recip", [128, TILES])
        by_score = sb("by_score", [128, TILES])
        by_half = sb("by_half", [128, TILES])
        gate_a = sb("gate_a", [128, TILES, E])
        gate_b = sb("gate_b", [128, TILES, E])
        gate = sb("gate", [128, TILES, E])
        logit = sb("logit", [E, N])
        gate_rows = logit
        gate_line = sb("gate_line", [1, 2, E, BLK])
        gate_wide = sb("gate_wide", [128, GRING, BLK])

        activated = sb("activated", [C, ARING, BLK])
        hidden = sb("hidden", [C, RING, BLK])
        hid_hi = sb("hid_hi", [C, RING, BLK], F32R)
        hid_lo = sb("hid_lo", [C, RING, BLK], F32R)
        zeros = hid_lo[:, RING - 1, :]
        partial = scaled
        result = xy

        up_ps = ctx.enter_context(nc.psum_tensor("up_ps", [128, 4, BLK], F32))
        acc_ps = ctx.enter_context(nc.psum_tensor("acc_ps", [128, 2, BLK], F32))
        misc_ps = ctx.enter_context(nc.psum_tensor("misc_ps", [128, 2, BLK], F32))
        mod_half_ps = [acc_ps[:, 0, 0:HALF], up_ps[:, 0, 0:HALF]]
        mod_ps = [None, acc_ps[:, 1, :], misc_ps[:, 0, :], misc_ps[:, 1, :]]
        demod_ps = up_ps[:, 2, 0:BATCH]
        batch_logit_ps = misc_ps[0:BPT, 1, 0:TILES * E].rearrange("p (t e) -> p t e", e=E)
        cond_logit_ps = misc_ps[:, 1, TILES * E:2 * TILES * E].rearrange("p (t e) -> p t e", e=E)
        logit_ps = misc_ps[:, 0, 0:TILES * E].rearrange("p (t e) -> p t e", e=E)

        in_cond, in_mod_w, in_small = sem("in_cond"), sem("in_mod_w"), sem("in_small")
        in_x0b = sem("in_x0b")
        in_x = [sem(f"in_x{b}") for b in range(NB)]
        in_up_s = [sem(f"in_up_s{h}") for h in range(2)]
        in_up_r, in_down_s, in_down_r = sem("in_up_r"), sem("in_down_s"), sem("in_down_r")
        up_hi_s, up_lo_s, down_hi_s, down_lo_s = sem("up_hi_s"), sem("up_lo_s"), sem("down_hi_s"), sem("down_lo_s")
        routed_hi, routed_lo = sem("routed_hi"), sem("routed_lo")
        zeros_ready = sem("zeros_ready")
        router_zero, router_hi_done, router_split = sem("router_zero"), sem("router_hi_done"), sem("router_split")
        ys_ready, squares_ready, demod_mm, demod_var_done = sem("ys_ready"), sem("squares_ready"), sem("demod_mm"), sem("demod_var_done")
        demod_inv_done, demod_ready = sem("demod_inv_done"), sem("demod_ready")
        xy_dve, xy_pool = sem("xy_dve"), sem("xy_pool")
        mod_mm, scaled_done, x1_done, x1_hi_done, x1_lo_dve, x1_lo_pool = (
            sem("mod_mm"), sem("scaled_done"), sem("x1_done"), sem("x1_hi_done"), sem("x1_lo_dve"), sem("x1_lo_pool"))
        batch_logit_mm, batch_logit_done = sem("batch_logit_mm"), sem("batch_logit_done")
        cond_logit_mm, cond_logit_done, logit_mm, logit_done, full_logit_done = (
            sem("cond_logit_mm"), sem("cond_logit_done"), sem("logit_mm"), sem("logit_done"), sem("full_logit_done"))
        logit_turned, score_done, router_chain = sem("logit_turned"), sem("score_done"), sem("router_chain")
        gate_turned, gate_rows_done, gate_wide_done = sem("gate_turned"), sem("gate_rows_done"), sem("gate_wide_done")
        gate_lined = sem("gate_lined")
        pre_ready, mul_ready, act_done, hidden_done = sem("pre_ready"), sem("mul_ready"), sem("act_done"), sem("hidden_done")
        hi_done, lo_dve, lo_pool, down_done = sem("hi_done"), sem("lo_dve"), sem("lo_pool"), sem("down_done")
        acc_taken, out_done = sem("acc_taken"), sem("out_done")

        SH = 2 * CH * C
        SD = CH * C

        routed_pieces = [(up_w, up_hi, SH + c * BLK) for c in range(E * C // BLK)]
        routed_pieces += [(down_w, down_hi, SD + c * BLK) for c in range(E * C // BLK)]

        def tok(b):
            return bass.ds(b * BLK, BLK)

        def by_batch(ap):
            return ap.rearrange("p (b s) -> p b s", s=SEQ)

        block = ctx.enter_context(nc.Block())

        def half(h):
            return bass.ds(h * HALF, HALF)

        def last_half(h):
            return bass.ds(N - BLK + h * HALF, HALF)

        def batches(t, at, n):
            return t[:, at:at + n].unsqueeze(2).broadcast_to([t.shape[0], n, SEQ])


        @block.sync
        def _(sp):
            sp.dma_start(cond[:], condT).then_inc(in_cond, 16)
            sp.dma_start(x[:, half(0)], xT[:, half(0)]).then_inc(in_x[0], 16)
            sp.dma_start(x[:, half(1)], xT[:, half(1)]).then_inc(in_x0b, 16)
            sp.dma_start(up_w[:, SH // 2:SH], w_up[:, SH // 2:SH]).then_inc(in_up_s[1], 16)
            for b in range(1, NB):
                sp.dma_start(x[:, tok(b)], xT[:, tok(b)]).then_inc(in_x[b], 16)
            sp.dma_start(up_w[:, SH:], w_up[:, SH:]).then_inc(in_up_r, 16)
            sp.dma_start(down_w[:, SD:], w_down[:, SD:]).then_inc(in_down_r, 16)
            for b in range(NB):
                sp.wait_ge(gate_rows_done, b + 1)
                if b >= 1:
                    sp.wait_ge(gate_lined, 16 * b)
                if b >= 2:
                    sp.wait_ge(gate_wide_done, E * (b - 1))
                sp.dma_start(gate_line[0:1, b % 2], gate_rows[:, tok(b)]).then_inc(gate_lined, 16)
            for b in range(NB - 1):
                sp.wait_ge(acc_taken, NB + b + 1)
                sp.dma_start(outT[:, tok(b)], result[:, tok(b)]).then_inc(out_done, 16)
            sp.wait_ge(acc_taken, 2 * NB)
            sp.dma_start(outT[:, last_half(0)], result[:, last_half(0)]).then_inc(out_done, 16)
            sp.wait_ge(out_done, 16 * (NB + 1))

        @block.scalar
        def _(act):
            act.dma_start(mod_w[:], w0).then_inc(in_mod_w, 16)
            act.dma_start(small[:], small_rows).then_inc(in_small, 16)
            act.dma_start(up_w[:, 0:SH // 2], w_up[:, 0:SH // 2]).then_inc(in_up_s[0], 16)
            act.dma_start(down_w[:, 0:SD], w_down[:, 0:SD]).then_inc(in_down_s, 16)

            def copy(out, in_):
                return nc.scalar.activation(out, in_, ACT.Copy)

            act.wait_ge(demod_inv_done, 1)
            nc.scalar.activation(demod[:], demod_inv[:], ACT.Sqrt).then_inc(demod_ready, 1)

            def up_high(c):
                part = bass.ds(c * SH // 2, SH // 2)
                act.wait_ge(in_up_s[c], 16)
                copy(up_hi[:, part], up_w[:, part]).then_inc(up_hi_s, 1)

            up_high(0)
            for h in range(2):
                act.wait_ge(x1_done, h + 1)
                copy(x1_hi[:, half(h)], x1[:, half(h)]).then_inc(x1_hi_done, 1)

            def high(buf, n):
                act.wait_ge(hidden_done, n + 1)
                copy(hid_hi[:, buf, :], hidden[:, buf, :]).then_inc(hi_done, 1)

            for n in range(NS):
                act.wait_ge(pre_ready, n + 1)
                if n >= ARING:
                    act.wait_ge(hidden_done, n - ARING + 1)
                nc.scalar.activation(activated[:, n % ARING, :], up_ps[:, 2 * (n % 2), :], ACT.Silu).then_inc(act_done, 1)
                if n == 0:
                    up_high(1)
                    act.wait_ge(in_down_s, 16)
                    copy(down_hi[:, 0:SD], down_w[:, 0:SD]).then_inc(down_hi_s, 1)
                elif n < NB:
                    act.wait_ge(x1_done, n + 2)
                    copy(x1_hi[:, tok(n)], x1[:, tok(n)]).then_inc(x1_hi_done, 1)
                if n >= 1:
                    high((n - 1) % RING, n - 1)
                for b in LOGITS_AFTER.get(n, ()):
                    act.wait_ge(logit_mm, b + 1)
                    copy(logit[:, tok(b)], misc_ps[0:E, b % 2, :]).then_inc(logit_done, 1)
                if n == TURN_AFTER + 1:
                    act.wait_ge(full_logit_done, 1)
                    nc.scalar.activation(score[:], full_logit[:], ACT.Sigmoid).then_inc(score_done, 1)
                if n in SPLIT_AFTER:
                    full, upper, at = routed_pieces[SPLIT_AFTER.index(n)]
                    if n == SPLIT_AFTER[0]:
                        act.wait_ge(in_up_r, 16)
                        act.wait_ge(in_down_r, 16)
                    copy(upper[:, bass.ds(at, BLK)], full[:, bass.ds(at, BLK)]).then_inc(routed_hi, 1)
                if n >= NS - 2:
                    for b in (2 * (n - NS + 2), 2 * (n - NS + 2) + 1):
                        act.wait_ge(gate_turned, b + 1)
                        copy(gate_rows[:, tok(b)], misc_ps[0:E, b % 2, :]).then_inc(gate_rows_done, 1)

            with act.Fori(0, NB // 2) as pair:
                for e in range(2 * E):
                    n = NS + 2 * E * pair + e
                    act.wait_ge(pre_ready, n + 1)
                    act.wait_ge(hidden_done, n - ARING + 1)
                    nc.scalar.activation(activated[:, e % ARING, :], up_ps[:, e % 4, :], ACT.Gelu).then_inc(act_done, 1)
                    high((e - 1) % RING, n - 1)
            high((E - 1) % RING, NS + NB * E - 1)
            act.wait_ge(acc_taken, 2 * NB + 1)
            act.dma_start(outT[:, last_half(1)], result[:, last_half(1)]).then_inc(out_done, 16)

        @block.vector
        def _(dve):
            def mult(out, a, b):
                return nc.vector.tensor_tensor(out, a, b, ALU.mult)

            def sub(out, a, b):
                return nc.vector.tensor_tensor(out, a, b, ALU.subtract)

            nc.vector.memset(zeros.bitcast(F32), 0.0).then_inc(zeros_ready, 1)
            dve.wait_ge(in_cond, 16)
            nc.vector.tensor_scalar(ys[:], cond[:], XSCALE, None, ALU.mult).then_inc(ys_ready, 1)
            dve.wait_ge(ys_ready, 1)
            mult(ys_sq[:], ys[:], ys[:]).then_inc(squares_ready, 1)
            dve.wait_ge(in_mod_w, 16)
            mult(mod_sq[:], mod_w[:], mod_w[:]).then_inc(squares_ready, 1)
            for h in range(2):
                dve.wait_ge(in_x0b if h else in_x[0], 16)
                mult(by_batch(xy[:, half(h)]), by_batch(x[:, half(h)]),
                     batches(ys, h * BPB // 2, BPB // 2)).then_inc(xy_dve, 1)
            dve.wait_ge(demod_mm, 1)
            nc.vector.tensor_scalar(demod_var[:], demod_ps, EPS, None, ALU.add).then_inc(demod_var_done, 1)
            dve.wait_ge(demod_var_done, 1)
            nc.vector.reciprocal(demod_inv[:], demod_var[:]).then_inc(demod_inv_done, 1)
            dve.wait_ge(demod_ready, 1)

            def residual(part, mod, first_batch, count):
                dve.wait_ge(mod_mm, count)
                mult(by_batch(scaled[:, part]), by_batch(mod),
                     batches(demod, first_batch, mod.shape[1] // SEQ)).then_inc(scaled_done, 1)
                dve.wait_ge(scaled_done, count)
                nc.vector.tensor_tensor(x1[:, part], scaled[:, part], x[:, part], ALU.add).then_inc(x1_done, 1)

            for h in range(2):
                residual(half(h), mod_half_ps[h], h * BPB // 2, h + 1)
            for h in range(2):
                dve.wait_ge(x1_hi_done, h + 1)
                sub(x1_lo[:, half(h)], x1[:, half(h)], x1_hi[:, half(h)]).then_inc(x1_lo_dve, 1)
            dve.wait_ge(in_x[1], 16)
            mult(by_batch(xy[:, tok(1)]), by_batch(x[:, tok(1)]), batches(ys, BPB, BPB)).then_inc(xy_dve, 1)
            dve.wait_ge(batch_logit_mm, 1)
            nc.vector.tensor_copy(batch_logit[:], batch_logit_ps).then_inc(batch_logit_done, 1)

            def wide(ap):
                return ap.unsqueeze(2).broadcast_to([128, TILES, E])

            def rows(ap):
                return ap.unsqueeze(1).broadcast_to([128, TILES, E])

            def pick_best(k, values):
                yield nc.vector.tensor_reduce(best[:, k, :], values[:], AX_X, ALU.max)
                yield nc.vector.tensor_tensor(is_best[:, k], values[:], wide(best[:, k, :]), ALU.is_equal)
                yield mult(ranked[:, k], is_best[:, k], rows(order))
                yield nc.vector.tensor_reduce(rank[:, k, :], ranked[:, k], AX_X, ALU.max)
                yield nc.vector.tensor_tensor(pick[:, k], rows(order), wide(rank[:, k, :]), ALU.is_equal)

            def gate_operations():
                yield nc.vector.tensor_tensor(biased[:], score[:], rows(bias), ALU.add)
                yield from pick_best(0, biased)
                yield nc.vector.scalar_tensor_tensor(rest[:], pick[:, 0], FAR, biased[:], ALU.mult, ALU.add)
                yield from pick_best(1, rest)
                yield nc.vector.tensor_tensor(picked[:], pick[:, 0], pick[:, 1], ALU.add)
                yield mult(kept[:], score[:], picked[:])
                yield nc.vector.tensor_reduce(denom[:], kept[:], AX_X, ALU.add)
                yield nc.vector.tensor_scalar(usable[:], denom[:], 1e-9, None, ALU.is_gt)
                yield nc.vector.tensor_scalar(denom_eps[:], denom[:], 1e-9, None, ALU.add)
                yield nc.vector.reciprocal(recip[:], denom_eps[:])
                yield mult(by_score[:], recip[:], usable[:])
                yield nc.vector.tensor_scalar(by_half[:], usable[:], -0.5, 0.5, ALU.mult, ALU.add)
                yield mult(gate_a[:], kept[:], wide(by_score[:]))
                yield mult(gate_b[:], picked[:], wide(by_half[:]))
                yield nc.vector.tensor_tensor(gate[:], gate_a[:], gate_b[:], ALU.add)

            gates = gate_operations()
            made = [0]

            def gate_step(times=1):
                for _ in range(times):
                    if made[0] < GATE_OPS:
                        if made[0]:
                            dve.wait_ge(router_chain, made[0])
                        next(gates).then_inc(router_chain, 1)
                        made[0] += 1

            def take_shared(b):
                dve.wait_ge(down_done, CH * (b + 1))
                nc.vector.scalar_tensor_tensor(partial[:, tok(b)], acc_ps[:, b % 2, :], 0.125, x1[:, tok(b)],
                                               ALU.mult, ALU.add).then_inc(acc_taken, 1)

            def low(buf, n):
                dve.wait_ge(hi_done, n + 1)
                sub(hid_lo[:, buf, :], hidden[:, buf, :], hid_hi[:, buf, :]).then_inc(lo_dve, 1)

            for n in range(NS):
                in_gates = n >= TURN_AFTER + 2
                if n == TURN_AFTER + 2:
                    dve.wait_ge(score_done, 1)
                if in_gates:
                    gate_step(2)
                dve.wait_ge(act_done, n + 1)
                dve.wait_ge(mul_ready, n + 1)
                mult(hidden[:, n % RING, :], activated[:, n % ARING, :], up_ps[:, 2 * (n % 2) + 1, :]).then_inc(hidden_done, 1)
                if n + 1 < NB:
                    residual(tok(n + 1), mod_ps[n + 1], (n + 1) * BPB, n + 3)
                if n == 0:
                    dve.wait_ge(cond_logit_mm, 1)
                    nc.vector.tensor_copy(cond_logit[:], cond_logit_ps).then_inc(cond_logit_done, 1)
                if in_gates:
                    gate_step()
                for m in LOW_AFTER.get(n, ()):
                    low(m % RING, m)
                if in_gates and n not in LOW_AFTER:
                    gate_step(2)
                if n == TURN_AFTER + 1:
                    dve.wait_ge(logit_turned, 1)
                    dve.wait_ge(cond_logit_done, 1)
                    nc.vector.tensor_tensor(full_logit[:], logit_ps, cond_logit[:], ALU.add).then_inc(full_logit_done, 1)
                if in_gates:
                    gate_step()
                if n >= CH + SKEW and (n - SKEW) % CH == 0:
                    take_shared((n - SKEW) // CH - 1)
            gate_step(GATE_OPS)

            def routed_step(b, e):
                n = NS + E * b + e
                dve.wait_ge(gate_wide_done, E * b + e + 1)
                dve.wait_ge(act_done, n + 1)
                mult(hidden[:, e % RING, :], activated[:, e % ARING, :], gate_wide[:, e % GRING, :]).then_inc(hidden_done, 1)
                if (e - 1) % E not in POOL_EXPERTS:
                    low((e - 1) % RING, n - 1)

            def take_routed(b):
                dve.wait_ge(down_done, NS + E * (b + 1))
                nc.vector.scalar_tensor_tensor(result[:, tok(b)], acc_ps[:, b % 2, :], 0.25, partial[:, tok(b)],
                                               ALU.mult, ALU.add).then_inc(acc_taken, 1)

            for e in range(E):
                routed_step(0, e)
                if (NS + e - SKEW) % CH == 0 and (NS + e - SKEW) // CH <= NB:
                    take_shared((NS + e - SKEW) // CH - 1)
            with dve.Fori(1, NB) as b:
                for e in range(E):
                    routed_step(b, e)
                    if e == SKEW:
                        take_routed(b - 1)
            low((E - 1) % RING, NS + NB * E - 1)
            dve.wait_ge(down_done, NS + E * NB)
            for h in range(2):
                nc.vector.scalar_tensor_tensor(result[:, last_half(h)], acc_ps[:, (NB - 1) % 2, half(h)], 0.25,
                                               partial[:, last_half(h)], ALU.mult, ALU.add).then_inc(acc_taken, 1)

        @block.gpsimd
        def _(pool):
            def sub(out, full, upper):
                return nc.gpsimd.tensor_tensor(out, full, upper, ALU.subtract)

            nc.gpsimd.memset(router_hi[:].bitcast(F32), 0.0)
            nc.gpsimd.memset(router_lo[:].bitcast(F32), 0.0).then_inc(router_zero, 1)

            def up_low(c):
                part = bass.ds(c * 2 * C, 2 * C)
                sub(up_lo[:, part], up_w[:, part], up_hi[:, part]).then_inc(up_lo_s, 1)

            def modulate(b):
                pool.wait_ge(in_x[b], 16)
                nc.gpsimd.tensor_tensor(by_batch(xy[:, tok(b)]), by_batch(x[:, tok(b)]), batches(ys, b * BPB, BPB),
                                        ALU.mult).then_inc(xy_pool, 1)

            pool.wait_ge(up_hi_s, 1)
            up_low(0)
            up_low(1)
            pool.wait_ge(ys_ready, 1)
            modulate(2)
            modulate(3)
            pool.wait_ge(up_hi_s, 2)
            up_low(2)
            up_low(3)
            pool.wait_ge(in_small, 16)
            pool.wait_ge(router_zero, 1)
            nc.gpsimd.tensor_copy(router_hi[:, 0:E], router_w[:, 0:E]).then_inc(router_hi_done, 1)
            for b in range(1, NB):
                pool.wait_ge(x1_hi_done, b + 2)
                sub(x1_lo[:, tok(b)], x1[:, tok(b)], x1_hi[:, tok(b)]).then_inc(x1_lo_pool, 1)
                if b == 2:
                    pool.wait_ge(down_hi_s, 1)
                    sub(down_lo[:, 0:SD], down_w[:, 0:SD], down_hi[:, 0:SD]).then_inc(down_lo_s, 1)
                if b == 1:
                    pool.wait_ge(router_hi_done, 1)
                    sub(router_lo[:, 0:E], router_w[:, 0:E], router_hi[:, 0:E]).then_inc(router_split, 1)
            def low(n):
                pool.wait_ge(hi_done, n + 1)
                sub(hid_lo[:, n % RING, :], hidden[:, n % RING, :], hid_hi[:, n % RING, :]).then_inc(lo_pool, 1)

            for n in range(NS):
                if low_on_pool(n):
                    low(n)
                if n - 1 in LOWS_AFTER:
                    piece = LOWS_AFTER.index(n - 1)
                    full, upper, at = routed_pieces[piece]
                    lower = up_lo if full is up_w else down_lo
                    part = bass.ds(at, BLK)
                    pool.wait_ge(routed_hi, piece + 1)
                    sub(lower[:, part], full[:, part], upper[:, part]).then_inc(routed_lo, 1)
            for m in range(NB * E):
                b, e = divmod(m, E)
                if m >= GRING + 1 and (m - GRING - 1) % E in POOL_EXPERTS:
                    low(NS + m - GRING - 1)
                if e == 0:
                    pool.wait_ge(gate_lined, 16 * (b + 1))
                if m >= GRING:
                    pool.wait_ge(hidden_done, NS + m - GRING + 1)
                nc.gpsimd.partition_broadcast(gate_wide[:, m % GRING, :], gate_line[0:1, b % 2, e, :]).then_inc(gate_wide_done, 1)
            for m in range(NB * E, NB * E + GRING + 1):
                if (m - GRING - 1) % E in POOL_EXPERTS:
                    low(NS + m - GRING - 1)

        @block.tensor
        def _(pe):
            def three_passes(out, w_hi, w_lo, v_hi, v_lo, first=True, last=True):
                nc.tensor.matmul(out, w_hi, v_hi, start=first, stop=False)
                nc.tensor.matmul(out, w_hi, v_lo, start=False, stop=False)
                return nc.tensor.matmul(out, w_lo, v_hi, start=False, stop=last)


            def modulated(b):
                nc.tensor.matmul(mod_ps[b], mod_w[:], xy[:, tok(b)], start=True, stop=True).then_inc(mod_mm, 1)

            def keep_busy(times):
                for _ in range(times):
                    nc.tensor.matmul(acc_ps[:, 1, :], zeros[:, 0:128], zeros, start=True, stop=True)

            pe.wait_ge(zeros_ready, 1)
            keep_busy(WARM_BEFORE)
            pe.wait_ge(squares_ready, 2)
            nc.tensor.matmul(demod_ps, mod_sq[:], ys_sq[:], start=True, stop=True).then_inc(demod_mm, 1)
            for h in range(2):
                pe.wait_ge(xy_dve, h + 1)
                nc.tensor.matmul(mod_half_ps[h], mod_w[:], xy[:, half(h)], start=True, stop=True).then_inc(mod_mm, 1)
            pe.wait_ge(in_small, 16)
            for t in range(TILES):
                last = nc.tensor.matmul(batch_logit_ps[:, t, :], cond[:, bass.ts(t, BPT)], router_w[:, E:2 * E],
                                        start=True, stop=True)
            last.then_inc(batch_logit_mm, 1)
            keep_busy(WARM_AFTER)
            def shared_up(n):
                b, j = divmod(n, CH)
                parts = [tok(b)]
                if n == 0:
                    parts = [half(0), half(1)]
                elif j == 0:
                    pe.wait_ge(x1_hi_done, b + 2)
                    pe.wait_ge(x1_lo_pool, b)
                if b == 0:
                    pe.wait_ge(up_lo_s, j + 1)
                if n >= 2:
                    pe.wait_ge(act_done, n - 1)
                if n == 1:
                    pe.wait_ge(demod_var_done, 1)
                for k, (ready, weights) in enumerate(((pre_ready, bass.ds(2 * j * C, C)), (mul_ready, bass.ds((2 * j + 1) * C, C)))):
                    if k == 1 and n >= 2:
                        pe.wait_ge(hidden_done, n - 1)
                    for h, part in enumerate(parts):
                        if n == 0 and k == 0:
                            pe.wait_ge(x1_lo_dve, h + 1)
                        out = up_ps[:, 2 * (n % 2) + k, half(h) if n == 0 else slice(0, BLK)]
                        last = three_passes(out, up_hi[:, weights], up_lo[:, weights], x1_hi[:, part], x1_lo[:, part])
                    last.then_inc(ready, 1)

            def down(out, weights, buf, first, last):
                three_passes(out, down_hi[:, weights], down_lo[:, weights],
                             hid_hi[:, buf, :], hid_lo[:, buf, :], first=first, last=last).then_inc(down_done, 1)

            def shared_down(n):
                b, j = divmod(n, CH)
                if n == 0:
                    pe.wait_ge(down_lo_s, 1)
                if j == 0:
                    if b < 2:
                        pe.wait_ge(scaled_done, b + 2)
                    else:
                        pe.wait_ge(acc_taken, b - 1)
                pe.wait_ge(hi_done, n + 1)
                if low_on_pool(n):
                    pe.wait_ge(lo_pool, sum(low_on_pool(i) for i in range(n + 1)))
                else:
                    pe.wait_ge(lo_dve, sum(not low_on_pool(i) for i in range(n + 1)))
                down(acc_ps[:, b % 2, :], bass.ts(j, C), n % RING, j == 0, j == CH - 1)

            def logits(b):
                if b > 0:
                    pe.wait_ge(x1_lo_pool, b)
                pe.wait_ge(router_split, 1)
                if b < 2:
                    pe.wait_ge(scaled_done, b + 4)
                else:
                    pe.wait_ge(logit_done, b - 1)
                three_passes(misc_ps[:, b % 2, :], router_hi[:], router_lo[:],
                             x1_hi[:, tok(b)], x1_lo[:, tok(b)]).then_inc(logit_mm, 1)

            def turn_gates(b):
                if b == 0:
                    pe.wait_ge(router_chain, GATE_OPS)
                if b >= 2:
                    pe.wait_ge(gate_rows_done, b - 1)
                for t in range(TPB):
                    last = nc.tensor.transpose(misc_ps[0:E, b % 2, bass.ts(t, 128)], gate[:, b * TPB + t, :], eye)
                last.then_inc(gate_turned, 1)

            for n in range(NS):
                shared_up(n)
                if n + 1 < NB:
                    if n == 0:
                        pe.wait_ge(xy_dve, 3)
                    else:
                        pe.wait_ge(xy_pool, n)
                    if n + 1 == 3:
                        pe.wait_ge(cond_logit_done, 1)
                    modulated(n + 1)
                if n == 0:
                    pe.wait_ge(batch_logit_done, 1)
                    nc.tensor.matmul(cond_logit_ps, own_batch, batch_logit[:], start=True, stop=True).then_inc(cond_logit_mm, 1)
                if n >= SKEW:
                    shared_down(n - SKEW)
                for b in LOGITS_AFTER.get(n, ()):
                    logits(b)
                if n == TURN_AFTER:
                    pe.wait_ge(logit_done, NB)
                    for t in range(TILES):
                        last = nc.tensor.transpose(logit_ps[:, t, :], logit[:, bass.ts(t, 128)], eye[0:E, 0:E])
                    last.then_inc(logit_turned, 1)
                if n >= NS - 2:
                    turn_gates(2 * (n - NS + 2))
                    turn_gates(2 * (n - NS + 2) + 1)

            def routed_up(b, e):
                w1 = bass.ds(SH + e * C, C)
                if isinstance(b, int) and e < 4:
                    pe.wait_ge(hidden_done, NS - 1 if e < 2 else NS)
                else:
                    pe.wait_ge(act_done, NS + E * b + e - 3)
                three_passes(up_ps[:, e % 4, :], up_hi[:, w1], up_lo[:, w1],
                             x1_hi[:, tok(b)], x1_lo[:, tok(b)]).then_inc(pre_ready, 1)

            def routed_down(b, e):
                if e == 0:
                    pe.wait_ge(acc_taken, NB + b - 1)
                pe.wait_ge(hi_done, NS + E * b + e + 1)
                if e in POOL_EXPERTS:
                    pe.wait_ge(lo_pool, POOL_LOWS + len(POOL_EXPERTS) * b + pool_experts(e))
                else:
                    pe.wait_ge(lo_dve, NS - POOL_LOWS + (E - len(POOL_EXPERTS)) * b + e + 1 - pool_experts(e))
                down(acc_ps[:, b % 2, :], bass.ds(SD + e * C, C), e % RING, e == 0, e == E - 1)

            pe.wait_ge(routed_lo, len(routed_pieces))
            for e in range(E):
                routed_up(0, e)
                if e < SKEW:
                    shared_down(NS - SKEW + e)
                else:
                    routed_down(0, e - SKEW)
            with pe.Fori(1, NB) as b:
                for e in range(E):
                    routed_up(b, e)
                    if e < SKEW:
                        routed_down(b - 1, E + e - SKEW)
                    else:
                        routed_down(b, e - SKEW)
            for e in range(E - SKEW, E):
                routed_down(NB - 1, e)


def kernel(**inputs):
    import numpy as np
    import concourse.bacc as bacc
    from concourse.bass_utils import run_bass_kernel_spmd

    a = {k: np.asarray(v) for k, v in inputs.items()}
    s_w1, s_w3 = (a[f"L1_cond_{k}"].reshape(CH, C, C) for k in ("s_w1", "s_w3"))
    s_w2 = a["L1_cond_s_w2"].reshape(2, C, 2, C).transpose(0, 2, 3, 1).reshape(CH * C, C)
    shared_up = np.stack([s_w1, s_w3], axis=1).reshape(2 * CH * C, C)
    routed_up = a["L1_cond_r_w1"].reshape(E * C, C)
    routed_down = a["L1_cond_r_w2"].transpose(0, 2, 1).reshape(E * C, C)
    down = np.concatenate([s_w2, routed_down]).reshape(CH + E, C, C).transpose(1, 0, 2)
    router = a["L1_cond_W_router"]
    arrays = {
        "xT": a["x"].reshape(N, C).T,
        "condT": a["cond_1024"].T,
        "w0": a["L0_cond_weight"],
        "w_up": np.concatenate([shared_up, routed_up]).T,
        "w_down": down.reshape(C, (CH + E) * C),
        "small_rows": np.concatenate([
            router[:, :C].T, router[:, C:].T,
            np.broadcast_to(a["L1_cond_router_bias"], (128, E)),
            np.broadcast_to(np.arange(E, 0, -1, dtype=np.float32), (128, E)),
            np.eye(128, dtype=np.float32),
            np.tile(np.repeat(np.eye(BPT, dtype=np.float32), SEQ, axis=1), (128 // BPT, 1))], axis=1),
    }
    arrays = {k: np.ascontiguousarray(v) for k, v in arrays.items()}
    nc = bacc.Bacc("TRN2", target_bir_lowering=False, num_devices=1)
    args = [nc.dram_tensor(k, v.shape, mybir.dt.from_np(v.dtype), kind="ExternalInput").ap() for k, v in arrays.items()]
    out = nc.dram_tensor("outT", (C, N), F32, kind="ExternalOutput").ap()
    build(nc, *args, out)
    r = run_bass_kernel_spmd(nc, [arrays], core_ids=[0])
    return r.results[0]["outT"].T.reshape(BATCH, SEQ, C)
```

```python
from contextlib import ExitStack

import concourse.bass as bass
from concourse import mybir

F32 = mybir.dt.float32
F32R = mybir.dt.float32r
ALU = mybir.AluOpType
ACT = mybir.ActivationFunctionType
AX_X = mybir.AxisListType.X

C = 128
BATCH = 64
SEQ = 32
N = BATCH * SEQ
BLK = 512
NB = N // BLK
BPB = BLK // SEQ
TILES = N // 128
TPB = BLK // 128
BPT = 128 // SEQ
E = 8
CH = 4
NS = NB * CH
RING = 8
ARING = 4
GRING = 4
SKEW = 5
PAD = E * (NB - 1)
HALF = BLK // 2
EPS = 1e-8
XSCALE = float(C) ** -0.5
FAR = -3.0e38
WARM_BEFORE = 6
WARM_AFTER = 3
GATES_AFTER = 14
LOGITS_AFTER = {3: (0,), 4: (1,), 5: (2, 3)}
TURN_AFTER = 6
GATE_OPS = 23
GATE_PLAN = {8: (3, 1, 0), 9: (1, 1, 2), 10: (1, 1, 1), 11: (2, 2, 3), 12: (2, 2, 1)}
SPLIT_AFTER = [5, 6, 9, 11]
LOWS_AFTER = [6, 8, 10, 12]

POOL_EXPERTS = (2, 5)


def low_on_pool(n):
    return n % 2 == 0 and n >= 4


def pool_experts(e):
    return sum(i <= e for i in POOL_EXPERTS)


LOW_AFTER = {3: (0, 1), 4: (2,), 5: (3,)} | {n + 1: (n,) for n in range(NB, NS - 1) if not low_on_pool(n)}
assert sum(map(sum, GATE_PLAN.values())) == GATE_OPS
POOL_LOWS = sum(low_on_pool(n) for n in range(NS))


def build(nc, xT, condT, w0, w_up, w_down, small_rows, outT):
    with ExitStack() as ctx:
        def sb(name, shape, dt=F32):
            return ctx.enter_context(nc.sbuf_tensor(name, shape, dt))

        def sem(name):
            return ctx.enter_context(nc.semaphore(name))

        x = sb("x", [C, N])
        cond = sb("cond", [C, BATCH])
        mod_w = sb("mod_w", [C, C])
        up_w = sb("up_w", [C, (2 * CH + E) * C])
        up_hi = sb("up_hi", [C, (2 * CH + E) * C], F32R)
        up_lo = sb("up_lo", [C, (2 * CH + E) * C], F32R)
        down_w = sb("down_w", [C, (CH + E) * C])
        down_hi = sb("down_hi", [C, (CH + E) * C], F32R)
        down_lo = sb("down_lo", [C, (CH + E) * C], F32R)
        small = sb("small", [128, 4 * E + 256 + NB * E])
        router_w = small[:, 0:2 * E]
        bias = small[:, 2 * E:3 * E]
        order = small[:, 3 * E:4 * E]
        eye = small[:, 4 * E:4 * E + 128]
        own_batch = small[0:BPT, 4 * E + 128:4 * E + 256]
        both_shares = small[0:2 * NB * E, 4 * E + 256:]
        router_both = sb("router_both", [C, PAD + 128], F32R)
        router_hi = sb("router_hi", [C, PAD + 128], F32R)

        ys = sb("ys", [C, BATCH])
        ys_sq = sb("ys_sq", [C, BATCH])
        mod_sq = sb("mod_sq", [C, C])
        demod_var = sb("demod_var", [C, BATCH])
        demod_inv = sb("demod_inv", [C, BATCH])
        demod = sb("demod", [C, BATCH])
        xy = sb("xy", [C, N])
        scaled = sb("scaled", [C, N])
        x1 = sb("x1", [C, N])
        x1_hi = sb("x1_hi", [C, N], F32R)
        x1_lo = sb("x1_lo", [C, N], F32R)

        batch_logit = sb("batch_logit", [BPT, TILES, E])
        cond_logit = sb("cond_logit", [128, TILES, E])
        full_logit = sb("full_logit", [128, TILES, E])
        score = sb("score", [128, TILES, E])
        biased = sb("biased", [128, TILES, E])
        rest = sb("rest", [128, TILES, E])
        best = sb("best", [128, 2, TILES])
        is_best = sb("is_best", [128, 2, TILES, E])
        ranked = sb("ranked", [128, 2, TILES, E])
        rank = sb("rank", [128, 2, TILES])
        pick = sb("pick", [128, 2, TILES, E])
        picked = sb("picked", [128, TILES, E])
        kept = sb("kept", [128, TILES, E])
        denom = sb("denom", [128, TILES])
        usable = sb("usable", [128, TILES])
        denom_eps = sb("denom_eps", [128, TILES])
        recip = sb("recip", [128, TILES])
        by_score = sb("by_score", [128, TILES])
        by_half = sb("by_half", [128, TILES])
        gate_a = sb("gate_a", [128, TILES, E])
        gate_b = sb("gate_b", [128, TILES, E])
        gate = sb("gate", [128, NB, E, TPB])
        logit = sb("logit", [2 * NB * E, BLK])
        gate_rows = sb("gate_rows", [NB * E * TPB, 128])
        gate_line = sb("gate_line", [1, 2, E, BLK])
        gate_wide = sb("gate_wide", [128, GRING, BLK])

        activated = sb("activated", [C, ARING, BLK])
        hidden = sb("hidden", [C, RING, BLK])
        hid_hi = sb("hid_hi", [C, RING, BLK], F32R)
        hid_lo = sb("hid_lo", [C, RING, BLK], F32R)
        zeros = hid_lo[:, RING - 1, :]
        partial = scaled
        result = xy

        up_ps = ctx.enter_context(nc.psum_tensor("up_ps", [128, 4, BLK], F32))
        acc_ps = ctx.enter_context(nc.psum_tensor("acc_ps", [128, 2, BLK], F32))
        misc_ps = ctx.enter_context(nc.psum_tensor("misc_ps", [128, 2, BLK], F32))
        mod_half_ps = [acc_ps[:, 0, 0:HALF], up_ps[:, 0, 0:HALF]]
        mod_ps = [None, acc_ps[:, 1, :], misc_ps[:, 0, :], misc_ps[:, 1, :]]
        demod_ps = up_ps[:, 2, 0:BATCH]
        batch_logit_ps = misc_ps[0:BPT, 1, 0:TILES * E].rearrange("p (t e) -> p t e", e=E)
        cond_logit_ps = misc_ps[:, 1, TILES * E:2 * TILES * E].rearrange("p (t e) -> p t e", e=E)
        logit_rows_ps = misc_ps[:, 0, :]
        logit_ps = misc_ps[:, 1, 0:TILES * E].rearrange("p (t e) -> p t e", e=E)
        gate_rows_ps = misc_ps[:, 0, 0:128]

        in_cond, in_mod_w, in_small = sem("in_cond"), sem("in_mod_w"), sem("in_small")
        in_x0b = sem("in_x0b")
        in_x = [sem(f"in_x{b}") for b in range(NB)]
        in_up_s = [sem(f"in_up_s{h}") for h in range(2)]
        in_up_r, in_down_s, in_down_r = sem("in_up_r"), sem("in_down_s"), sem("in_down_r")
        up_hi_s, up_lo_s, down_hi_s, down_lo_s = sem("up_hi_s"), sem("up_lo_s"), sem("down_hi_s"), sem("down_lo_s")
        routed_hi, routed_lo = sem("routed_hi"), sem("routed_lo")
        zeros_ready = sem("zeros_ready")
        router_zero, router_hi_done, router_split = sem("router_zero"), sem("router_hi_done"), sem("router_split")
        ys_ready, squares_ready, demod_mm, demod_var_done = sem("ys_ready"), sem("squares_ready"), sem("demod_mm"), sem("demod_var_done")
        demod_inv_done, demod_ready = sem("demod_inv_done"), sem("demod_ready")
        xy_dve, xy_pool = sem("xy_dve"), sem("xy_pool")
        mod_mm, scaled_done, x1_done, x1_hi_done, x1_lo_dve, x1_lo_pool = (
            sem("mod_mm"), sem("scaled_done"), sem("x1_done"), sem("x1_hi_done"), sem("x1_lo_dve"), sem("x1_lo_pool"))
        batch_logit_mm, batch_logit_done = sem("batch_logit_mm"), sem("batch_logit_done")
        cond_logit_mm, cond_logit_done, logit_mm, logit_done, full_logit_done = (
            sem("cond_logit_mm"), sem("cond_logit_done"), sem("logit_mm"), sem("logit_done"), sem("full_logit_done"))
        logit_turned, score_done, router_chain = sem("logit_turned"), sem("score_done"), sem("router_chain")
        gate_turned, gate_rows_done, gate_wide_done = sem("gate_turned"), sem("gate_rows_done"), sem("gate_wide_done")
        gate_lined = sem("gate_lined")
        pre_ready, mul_ready, act_done, hidden_done = sem("pre_ready"), sem("mul_ready"), sem("act_done"), sem("hidden_done")
        hi_done, lo_dve, lo_pool, down_done = sem("hi_done"), sem("lo_dve"), sem("lo_pool"), sem("down_done")
        acc_taken, out_done = sem("acc_taken"), sem("out_done")

        SH = 2 * CH * C
        SD = CH * C

        routed_pieces = [(up_w, up_hi, SH + c * BLK) for c in range(E * C // BLK)]
        routed_pieces += [(down_w, down_hi, SD + c * BLK) for c in range(E * C // BLK)]

        def tok(b):
            return bass.ds(b * BLK, BLK)

        def by_batch(ap):
            return ap.rearrange("p (b s) -> p b s", s=SEQ)

        block = ctx.enter_context(nc.Block())

        def half(h):
            return bass.ds(h * HALF, HALF)

        def last_half(h):
            return bass.ds(N - BLK + h * HALF, HALF)

        def batches(t, at, n):
            return t[:, at:at + n].unsqueeze(2).broadcast_to([t.shape[0], n, SEQ])


        @block.sync
        def _(sp):
            sp.dma_start(cond[:], condT).then_inc(in_cond, 16)
            sp.dma_start(x[:, half(0)], xT[:, half(0)]).then_inc(in_x[0], 16)
            sp.dma_start(x[:, half(1)], xT[:, half(1)]).then_inc(in_x0b, 16)
            sp.dma_start(up_w[:, SH // 2:SH], w_up[:, SH // 2:SH]).then_inc(in_up_s[1], 16)
            for b in range(1, NB):
                sp.dma_start(x[:, tok(b)], xT[:, tok(b)]).then_inc(in_x[b], 16)
            sp.dma_start(up_w[:, SH:], w_up[:, SH:]).then_inc(in_up_r, 16)
            sp.dma_start(down_w[:, SD:], w_down[:, SD:]).then_inc(in_down_r, 16)
            for b in range(NB):
                if b == 0:
                    sp.wait_ge(gate_rows_done, 1)
                if b >= 1:
                    sp.wait_ge(gate_lined, 16 * b)
                if b >= 2:
                    sp.wait_ge(gate_wide_done, E * (b - 1))
                sp.dma_start(gate_line[0:1, b % 2], gate_rows[bass.ts(b, E * TPB), :]).then_inc(gate_lined, 16)
            for b in range(NB - 1):
                sp.wait_ge(acc_taken, NB + b + 1)
                sp.dma_start(outT[:, tok(b)], result[:, tok(b)]).then_inc(out_done, 16)
            sp.wait_ge(acc_taken, 2 * NB)
            sp.dma_start(outT[:, last_half(0)], result[:, last_half(0)]).then_inc(out_done, 16)
            sp.wait_ge(out_done, 16 * (NB + 1))

        @block.scalar
        def _(act):
            act.dma_start(mod_w[:], w0).then_inc(in_mod_w, 16)
            act.dma_start(small[:], small_rows).then_inc(in_small, 16)
            act.dma_start(up_w[:, 0:SH // 2], w_up[:, 0:SH // 2]).then_inc(in_up_s[0], 16)
            act.dma_start(down_w[:, 0:SD], w_down[:, 0:SD]).then_inc(in_down_s, 16)

            def copy(out, in_):
                return nc.scalar.activation(out, in_, ACT.Copy)

            act.wait_ge(demod_inv_done, 1)
            nc.scalar.activation(demod[:], demod_inv[:], ACT.Sqrt).then_inc(demod_ready, 1)

            def up_high(c):
                part = bass.ds(c * SH // 2, SH // 2)
                act.wait_ge(in_up_s[c], 16)
                copy(up_hi[:, part], up_w[:, part]).then_inc(up_hi_s, 1)

            up_high(0)
            for h in range(2):
                act.wait_ge(x1_done, h + 1)
                copy(x1_hi[:, half(h)], x1[:, half(h)]).then_inc(x1_hi_done, 1)

            def high(buf, n):
                act.wait_ge(hidden_done, n + 1)
                copy(hid_hi[:, buf, :], hidden[:, buf, :]).then_inc(hi_done, 1)

            for n in range(NS):
                act.wait_ge(pre_ready, n + 1)
                if n >= ARING:
                    act.wait_ge(hidden_done, n - ARING + 1)
                nc.scalar.activation(activated[:, n % ARING, :], up_ps[:, 2 * (n % 2), :], ACT.Silu).then_inc(act_done, 1)
                if n == 0:
                    up_high(1)
                    act.wait_ge(in_down_s, 16)
                    copy(down_hi[:, 0:SD], down_w[:, 0:SD]).then_inc(down_hi_s, 1)
                elif n < NB:
                    act.wait_ge(x1_done, n + 2)
                    copy(x1_hi[:, tok(n)], x1[:, tok(n)]).then_inc(x1_hi_done, 1)
                if n >= 1:
                    high((n - 1) % RING, n - 1)
                if n == TURN_AFTER - 1:
                    act.wait_ge(logit_mm, 1)
                    copy(logit[:], logit_rows_ps[0:2 * NB * E, :]).then_inc(logit_done, 1)
                if n == TURN_AFTER + 1:
                    act.wait_ge(full_logit_done, 1)
                    nc.scalar.activation(score[:], full_logit[:], ACT.Sigmoid).then_inc(score_done, 1)
                if n in SPLIT_AFTER:
                    full, upper, at = routed_pieces[SPLIT_AFTER.index(n)]
                    if n == SPLIT_AFTER[0]:
                        act.wait_ge(in_up_r, 16)
                        act.wait_ge(in_down_r, 16)
                    copy(upper[:, bass.ds(at, BLK)], full[:, bass.ds(at, BLK)]).then_inc(routed_hi, 1)
                if n == GATES_AFTER:
                    act.wait_ge(gate_turned, 1)
                    copy(gate_rows[:], gate_rows_ps).then_inc(gate_rows_done, 1)

            with act.Fori(0, NB // 2) as pair:
                for e in range(2 * E):
                    n = NS + 2 * E * pair + e
                    act.wait_ge(pre_ready, n + 1)
                    act.wait_ge(hidden_done, n - ARING + 1)
                    nc.scalar.activation(activated[:, e % ARING, :], up_ps[:, e % 4, :], ACT.Gelu).then_inc(act_done, 1)
                    high((e - 1) % RING, n - 1)
            high((E - 1) % RING, NS + NB * E - 1)
            act.wait_ge(acc_taken, 2 * NB + 1)
            act.dma_start(outT[:, last_half(1)], result[:, last_half(1)]).then_inc(out_done, 16)

        @block.vector
        def _(dve):
            def mult(out, a, b):
                return nc.vector.tensor_tensor(out, a, b, ALU.mult)

            def sub(out, a, b):
                return nc.vector.tensor_tensor(out, a, b, ALU.subtract)

            nc.vector.memset(zeros.bitcast(F32), 0.0).then_inc(zeros_ready, 1)
            dve.wait_ge(in_cond, 16)
            nc.vector.tensor_scalar(ys[:], cond[:], XSCALE, None, ALU.mult).then_inc(ys_ready, 1)
            dve.wait_ge(ys_ready, 1)
            mult(ys_sq[:], ys[:], ys[:]).then_inc(squares_ready, 1)
            dve.wait_ge(in_mod_w, 16)
            mult(mod_sq[:], mod_w[:], mod_w[:]).then_inc(squares_ready, 1)

            def modulate_half(h):
                dve.wait_ge(in_x0b if h else in_x[0], 16)
                mult(by_batch(xy[:, half(h)]), by_batch(x[:, half(h)]),
                     batches(ys, h * BPB // 2, BPB // 2)).then_inc(xy_dve, 1)

            modulate_half(0)
            dve.wait_ge(demod_mm, 1)
            nc.vector.tensor_scalar(demod_var[:], demod_ps, EPS, None, ALU.add).then_inc(demod_var_done, 1)
            modulate_half(1)
            dve.wait_ge(demod_var_done, 1)
            nc.vector.reciprocal(demod_inv[:], demod_var[:]).then_inc(demod_inv_done, 1)
            dve.wait_ge(demod_ready, 1)

            def rescale(part, mod, first_batch, count):
                dve.wait_ge(mod_mm, count)
                mult(by_batch(scaled[:, part]), by_batch(mod),
                     batches(demod, first_batch, mod.shape[1] // SEQ)).then_inc(scaled_done, 1)

            def residual(part, count):
                dve.wait_ge(scaled_done, count)
                nc.vector.tensor_tensor(x1[:, part], scaled[:, part], x[:, part], ALU.add).then_inc(x1_done, 1)

            for h in range(2):
                rescale(half(h), mod_half_ps[h], h * BPB // 2, h + 1)
            for h in range(2):
                residual(half(h), h + 1)
            for h in range(2):
                dve.wait_ge(x1_hi_done, h + 1)
                sub(x1_lo[:, half(h)], x1[:, half(h)], x1_hi[:, half(h)]).then_inc(x1_lo_dve, 1)
            dve.wait_ge(in_x[1], 16)
            mult(by_batch(xy[:, tok(1)]), by_batch(x[:, tok(1)]), batches(ys, BPB, BPB)).then_inc(xy_dve, 1)
            dve.wait_ge(batch_logit_mm, 1)
            nc.vector.tensor_copy(batch_logit[:], batch_logit_ps).then_inc(batch_logit_done, 1)

            def wide(ap):
                return ap.unsqueeze(2).broadcast_to([128, TILES, E])

            def by_block(t):
                return t[:].rearrange("p (b t) e -> p b t e", t=TPB)

            def rows(ap):
                return ap.unsqueeze(1).broadcast_to([128, TILES, E])

            def pick_best(k, values):
                yield nc.vector.tensor_reduce(best[:, k, :], values[:], AX_X, ALU.max)
                yield nc.vector.tensor_tensor(is_best[:, k], values[:], wide(best[:, k, :]), ALU.is_equal)
                yield mult(ranked[:, k], is_best[:, k], rows(order))
                yield nc.vector.tensor_reduce(rank[:, k, :], ranked[:, k], AX_X, ALU.max)
                yield nc.vector.tensor_tensor(pick[:, k], rows(order), wide(rank[:, k, :]), ALU.is_equal)

            def gate_operations():
                yield nc.vector.tensor_tensor(biased[:], score[:], rows(bias), ALU.add)
                yield from pick_best(0, biased)
                yield nc.vector.scalar_tensor_tensor(rest[:], pick[:, 0], FAR, biased[:], ALU.mult, ALU.add)
                yield from pick_best(1, rest)
                yield nc.vector.tensor_tensor(picked[:], pick[:, 0], pick[:, 1], ALU.add)
                yield mult(kept[:], score[:], picked[:])
                yield nc.vector.tensor_reduce(denom[:], kept[:], AX_X, ALU.add)
                yield nc.vector.tensor_scalar(usable[:], denom[:], 1e-9, None, ALU.is_gt)
                yield nc.vector.tensor_scalar(denom_eps[:], denom[:], 1e-9, None, ALU.add)
                yield nc.vector.reciprocal(recip[:], denom_eps[:])
                yield mult(by_score[:], recip[:], usable[:])
                yield nc.vector.tensor_scalar(by_half[:], usable[:], -0.5, 0.5, ALU.mult, ALU.add)
                yield mult(gate_a[:], kept[:], wide(by_score[:]))
                yield mult(gate_b[:], picked[:], wide(by_half[:]))
                yield nc.vector.tensor_tensor(gate[:].rearrange("p b e t -> p b t e"), by_block(gate_a), by_block(gate_b), ALU.add)

            gates = gate_operations()
            made = [0]

            def gate_step(times):
                for _ in range(times):
                    if made[0]:
                        dve.wait_ge(router_chain, made[0])
                    next(gates).then_inc(router_chain, 1)
                    made[0] += 1

            def take_shared(b):
                dve.wait_ge(down_done, CH * (b + 1))
                nc.vector.scalar_tensor_tensor(partial[:, tok(b)], acc_ps[:, b % 2, :], 0.125, x1[:, tok(b)],
                                               ALU.mult, ALU.add).then_inc(acc_taken, 1)

            def low(buf, n):
                dve.wait_ge(hi_done, n + 1)
                sub(hid_lo[:, buf, :], hidden[:, buf, :], hid_hi[:, buf, :]).then_inc(lo_dve, 1)

            for n in range(NS):
                gates_first, gates_later, gates_last = GATE_PLAN.get(n, (0, 0, 0))
                if n == TURN_AFTER + 2:
                    dve.wait_ge(score_done, 1)
                gate_step(gates_first)
                dve.wait_ge(act_done, n + 1)
                dve.wait_ge(mul_ready, n + 1)
                mult(hidden[:, n % RING, :], activated[:, n % ARING, :], up_ps[:, 2 * (n % 2) + 1, :]).then_inc(hidden_done, 1)
                if n + 1 < NB:
                    rescale(tok(n + 1), mod_ps[n + 1], (n + 1) * BPB, n + 3)
                    residual(tok(n + 1), n + 3)
                if n == 0:
                    dve.wait_ge(cond_logit_mm, 1)
                    nc.vector.tensor_copy(cond_logit[:], cond_logit_ps).then_inc(cond_logit_done, 1)
                gate_step(gates_later)
                for m in LOW_AFTER.get(n, ()):
                    low(m % RING, m)
                if n == TURN_AFTER + 1:
                    dve.wait_ge(logit_turned, 1)
                    dve.wait_ge(cond_logit_done, 1)
                    nc.vector.tensor_tensor(full_logit[:], logit_ps, cond_logit[:], ALU.add).then_inc(full_logit_done, 1)
                gate_step(gates_last)
                if n >= CH + SKEW and (n - SKEW) % CH == 0:
                    take_shared((n - SKEW) // CH - 1)

            def routed_step(b, e):
                n = NS + E * b + e
                dve.wait_ge(gate_wide_done, E * b + e + 1)
                dve.wait_ge(act_done, n + 1)
                mult(hidden[:, e % RING, :], activated[:, e % ARING, :], gate_wide[:, e % GRING, :]).then_inc(hidden_done, 1)
                if (e - 1) % E not in POOL_EXPERTS:
                    low((e - 1) % RING, n - 1)

            def take_routed(b):
                dve.wait_ge(down_done, NS + E * (b + 1))
                nc.vector.scalar_tensor_tensor(result[:, tok(b)], acc_ps[:, b % 2, :], 0.25, partial[:, tok(b)],
                                               ALU.mult, ALU.add).then_inc(acc_taken, 1)

            for e in range(E):
                routed_step(0, e)
                if (NS + e - SKEW) % CH == 0 and (NS + e - SKEW) // CH <= NB:
                    take_shared((NS + e - SKEW) // CH - 1)
            with dve.Fori(1, NB) as b:
                for e in range(E):
                    routed_step(b, e)
                    if e == SKEW:
                        take_routed(b - 1)
            low((E - 1) % RING, NS + NB * E - 1)
            dve.wait_ge(down_done, NS + E * NB)
            for h in range(2):
                nc.vector.scalar_tensor_tensor(result[:, last_half(h)], acc_ps[:, (NB - 1) % 2, half(h)], 0.25,
                                               partial[:, last_half(h)], ALU.mult, ALU.add).then_inc(acc_taken, 1)

        @block.gpsimd
        def _(pool):
            def sub(out, full, upper):
                return nc.gpsimd.tensor_tensor(out, full, upper, ALU.subtract)

            nc.gpsimd.memset(router_hi[:].bitcast(F32), 0.0)
            nc.gpsimd.memset(router_both[:].bitcast(F32), 0.0).then_inc(router_zero, 1)

            def up_low(c):
                part = bass.ds(c * 2 * C, 2 * C)
                sub(up_lo[:, part], up_w[:, part], up_hi[:, part]).then_inc(up_lo_s, 1)

            def modulate(b):
                pool.wait_ge(in_x[b], 16)
                nc.gpsimd.tensor_tensor(by_batch(xy[:, tok(b)]), by_batch(x[:, tok(b)]), batches(ys, b * BPB, BPB),
                                        ALU.mult).then_inc(xy_pool, 1)

            pool.wait_ge(up_hi_s, 1)
            up_low(0)
            up_low(1)
            pool.wait_ge(ys_ready, 1)
            modulate(2)
            modulate(3)
            pool.wait_ge(up_hi_s, 2)
            up_low(2)
            up_low(3)
            pool.wait_ge(in_small, 16)
            pool.wait_ge(router_zero, 1)
            for table in (router_hi, router_both):
                nc.gpsimd.tensor_copy(table[:, PAD:PAD + E], router_w[:, 0:E]).then_inc(router_hi_done, 1)
            for b in range(1, NB):
                pool.wait_ge(x1_hi_done, b + 2)
                sub(x1_lo[:, tok(b)], x1[:, tok(b)], x1_hi[:, tok(b)]).then_inc(x1_lo_pool, 1)
                if b == 2:
                    pool.wait_ge(down_hi_s, 1)
                    sub(down_lo[:, 0:SD], down_w[:, 0:SD], down_hi[:, 0:SD]).then_inc(down_lo_s, 1)
                if b == 1:
                    pool.wait_ge(router_hi_done, 2)
                    sub(router_both[:, PAD + NB * E:PAD + NB * E + E], router_w[:, 0:E], router_hi[:, PAD:PAD + E]).then_inc(router_split, 1)
            def low(n):
                pool.wait_ge(hi_done, n + 1)
                sub(hid_lo[:, n % RING, :], hidden[:, n % RING, :], hid_hi[:, n % RING, :]).then_inc(lo_pool, 1)

            for n in range(NS):
                if low_on_pool(n):
                    low(n)
                if n - 1 in LOWS_AFTER:
                    piece = LOWS_AFTER.index(n - 1)
                    full, upper, at = routed_pieces[piece]
                    lower = up_lo if full is up_w else down_lo
                    part = bass.ds(at, BLK)
                    pool.wait_ge(routed_hi, piece + 1)
                    sub(lower[:, part], full[:, part], upper[:, part]).then_inc(routed_lo, 1)
            for m in range(NB * E):
                b, e = divmod(m, E)
                if m >= GRING + 1 and (m - GRING - 1) % E in POOL_EXPERTS:
                    low(NS + m - GRING - 1)
                if e == 0:
                    pool.wait_ge(gate_lined, 16 * (b + 1))
                if m >= GRING:
                    pool.wait_ge(hidden_done, NS + m - GRING + 1)
                nc.gpsimd.partition_broadcast(gate_wide[:, m % GRING, :], gate_line[0:1, b % 2, e, :]).then_inc(gate_wide_done, 1)
            for m in range(NB * E, NB * E + GRING + 1):
                if (m - GRING - 1) % E in POOL_EXPERTS:
                    low(NS + m - GRING - 1)

        @block.tensor
        def _(pe):
            def three_passes(out, w_hi, w_lo, v_hi, v_lo, first=True, last=True):
                nc.tensor.matmul(out, w_hi, v_hi, start=first, stop=False)
                nc.tensor.matmul(out, w_hi, v_lo, start=False, stop=False)
                return nc.tensor.matmul(out, w_lo, v_hi, start=False, stop=last)

            def modulated(b):
                nc.tensor.matmul(mod_ps[b], mod_w[:], xy[:, tok(b)], start=True, stop=True).then_inc(mod_mm, 1)

            def keep_busy(times):
                for _ in range(times):
                    nc.tensor.matmul(acc_ps[:, 1, :], zeros[:, 0:128], zeros, start=True, stop=True)

            pe.wait_ge(zeros_ready, 1)
            keep_busy(WARM_BEFORE)
            pe.wait_ge(squares_ready, 2)
            nc.tensor.matmul(demod_ps, mod_sq[:], ys_sq[:], start=True, stop=True).then_inc(demod_mm, 1)
            for h in range(2):
                pe.wait_ge(xy_dve, h + 1)
                nc.tensor.matmul(mod_half_ps[h], mod_w[:], xy[:, half(h)], start=True, stop=True).then_inc(mod_mm, 1)
            pe.wait_ge(in_small, 16)
            for t in range(TILES):
                last = nc.tensor.matmul(batch_logit_ps[:, t, :], cond[:, bass.ts(t, BPT)], router_w[:, E:2 * E],
                                        start=True, stop=True)
            last.then_inc(batch_logit_mm, 1)
            keep_busy(WARM_AFTER)

            def shared_up(n):
                b, j = divmod(n, CH)
                if n > 0 and j == 0:
                    pe.wait_ge(x1_hi_done, b + 2)
                    pe.wait_ge(x1_lo_pool, b)
                if b == 0:
                    pe.wait_ge(up_lo_s, j + 1)
                if n >= 2:
                    pe.wait_ge(act_done, n - 1)
                if n == 1:
                    pe.wait_ge(demod_var_done, 1)
                w1, w3 = bass.ds(2 * j * C, C), bass.ds((2 * j + 1) * C, C)
                if n == 0:
                    for h in range(2):
                        pe.wait_ge(x1_lo_dve, h + 1)
                        for k, (ready, weights) in enumerate(((pre_ready, w1), (mul_ready, w3))):
                            last = three_passes(up_ps[:, k, half(h)], up_hi[:, weights], up_lo[:, weights],
                                                x1_hi[:, half(h)], x1_lo[:, half(h)])
                            if h == 1:
                                last.then_inc(ready, 1)
                    return
                three_passes(up_ps[:, 2 * (n % 2), :], up_hi[:, w1], up_lo[:, w1],
                             x1_hi[:, tok(b)], x1_lo[:, tok(b)]).then_inc(pre_ready, 1)
                if n >= 2:
                    pe.wait_ge(hidden_done, n - 1)
                three_passes(up_ps[:, 2 * (n % 2) + 1, :], up_hi[:, w3], up_lo[:, w3],
                             x1_hi[:, tok(b)], x1_lo[:, tok(b)]).then_inc(mul_ready, 1)

            def down(out, weights, buf, first, last):
                three_passes(out, down_hi[:, weights], down_lo[:, weights],
                             hid_hi[:, buf, :], hid_lo[:, buf, :], first=first, last=last).then_inc(down_done, 1)

            def shared_down(n):
                b, j = divmod(n, CH)
                if n == 0:
                    pe.wait_ge(down_lo_s, 1)
                if j == 0:
                    if b < 2:
                        pe.wait_ge(scaled_done, b + 2)
                    else:
                        pe.wait_ge(acc_taken, b - 1)
                pe.wait_ge(hi_done, n + 1)
                if low_on_pool(n):
                    pe.wait_ge(lo_pool, sum(low_on_pool(i) for i in range(n + 1)))
                else:
                    pe.wait_ge(lo_dve, sum(not low_on_pool(i) for i in range(n + 1)))
                down(acc_ps[:, b % 2, :], bass.ts(j, C), n % RING, j == 0, j == CH - 1)

            def logits(b):
                if b > 0:
                    pe.wait_ge(x1_lo_pool, b)
                if b == 0:
                    pe.wait_ge(router_split, 1)
                    pe.wait_ge(scaled_done, 4)
                window = bass.ds(PAD - E * b, 128)
                nc.tensor.matmul(logit_rows_ps, router_both[:, window], x1_hi[:, tok(b)], start=b == 0, stop=False)
                last = nc.tensor.matmul(logit_rows_ps, router_hi[:, window], x1_lo[:, tok(b)],
                                        start=False, stop=b == NB - 1)
                if b == NB - 1:
                    last.then_inc(logit_mm, 1)

            def turn_logits():
                pe.wait_ge(logit_done, 1)
                pe.wait_ge(scaled_done, 5)
                turned = logit_ps.rearrange("p (b t) e -> p t b e", t=TPB)
                for t in range(TPB):
                    last = nc.tensor.matmul(turned[:, t], logit[:, bass.ts(t, 128)], both_shares, start=True, stop=True)
                last.then_inc(logit_turned, 1)

            def turn_gates():
                pe.wait_ge(router_chain, GATE_OPS)
                nc.tensor.transpose(gate_rows_ps, gate[:].rearrange("p b e t -> p (b e t)"), eye).then_inc(gate_turned, 1)

            for n in range(NS):
                shared_up(n)
                if n + 1 < NB:
                    if n == 0:
                        pe.wait_ge(xy_dve, 3)
                    else:
                        pe.wait_ge(xy_pool, n)
                    if n + 1 == 3:
                        pe.wait_ge(cond_logit_done, 1)
                    modulated(n + 1)
                if n == 0:
                    pe.wait_ge(batch_logit_done, 1)
                    nc.tensor.matmul(cond_logit_ps, own_batch, batch_logit[:], start=True, stop=True).then_inc(cond_logit_mm, 1)
                if n >= SKEW:
                    shared_down(n - SKEW)
                for b in LOGITS_AFTER.get(n, ()):
                    logits(b)
                if n == TURN_AFTER:
                    turn_logits()
                if n == GATES_AFTER:
                    turn_gates()

            def routed_up(b, e):
                w1 = bass.ds(SH + e * C, C)
                if isinstance(b, int) and e < 4:
                    pe.wait_ge(hidden_done, NS - 1 if e < 2 else NS)
                else:
                    pe.wait_ge(act_done, NS + E * b + e - 3)
                three_passes(up_ps[:, e % 4, :], up_hi[:, w1], up_lo[:, w1],
                             x1_hi[:, tok(b)], x1_lo[:, tok(b)]).then_inc(pre_ready, 1)

            def routed_down(b, e):
                if e == 0:
                    pe.wait_ge(acc_taken, NB + b - 1)
                pe.wait_ge(hi_done, NS + E * b + e + 1)
                if e in POOL_EXPERTS:
                    pe.wait_ge(lo_pool, POOL_LOWS + len(POOL_EXPERTS) * b + pool_experts(e))
                else:
                    pe.wait_ge(lo_dve, NS - POOL_LOWS + (E - len(POOL_EXPERTS)) * b + e + 1 - pool_experts(e))
                down(acc_ps[:, b % 2, :], bass.ds(SD + e * C, C), e % RING, e == 0, e == E - 1)

            pe.wait_ge(routed_lo, len(routed_pieces))
            for e in range(E):
                routed_up(0, e)
                if e < SKEW:
                    shared_down(NS - SKEW + e)
                else:
                    routed_down(0, e - SKEW)
            with pe.Fori(1, NB) as b:
                for e in range(E):
                    routed_up(b, e)
                    if e < SKEW:
                        routed_down(b - 1, E + e - SKEW)
                    else:
                        routed_down(b, e - SKEW)
            for e in range(E - SKEW, E):
                routed_down(NB - 1, e)


def kernel(**inputs):
    import numpy as np
    import concourse.bacc as bacc
    from concourse.bass_utils import run_bass_kernel_spmd

    a = {k: np.asarray(v) for k, v in inputs.items()}
    s_w1, s_w3 = (a[f"L1_cond_{k}"].reshape(CH, C, C) for k in ("s_w1", "s_w3"))
    s_w2 = a["L1_cond_s_w2"].reshape(2, C, 2, C).transpose(0, 2, 3, 1).reshape(CH * C, C)
    shared_up = np.stack([s_w1, s_w3], axis=1).reshape(2 * CH * C, C)
    routed_up = a["L1_cond_r_w1"].reshape(E * C, C)
    routed_down = a["L1_cond_r_w2"].transpose(0, 2, 1).reshape(E * C, C)
    down = np.concatenate([s_w2, routed_down]).reshape(CH + E, C, C).transpose(1, 0, 2)
    router = a["L1_cond_W_router"]
    arrays = {
        "xT": a["x"].reshape(N, C).T,
        "condT": a["cond_1024"].T,
        "w0": a["L0_cond_weight"],
        "w_up": np.concatenate([shared_up, routed_up]).T,
        "w_down": down.reshape(C, (CH + E) * C),
        "small_rows": np.concatenate([
            router[:, :C].T, router[:, C:].T,
            np.broadcast_to(a["L1_cond_router_bias"], (128, E)),
            np.broadcast_to(np.arange(E, 0, -1, dtype=np.float32), (128, E)),
            np.eye(128, dtype=np.float32),
            np.tile(np.repeat(np.eye(BPT, dtype=np.float32), SEQ, axis=1), (128 // BPT, 1)),
            np.tile(np.eye(NB * E, dtype=np.float32), (128 // (NB * E), 1))], axis=1),
    }
    arrays = {k: np.ascontiguousarray(v) for k, v in arrays.items()}
    nc = bacc.Bacc("TRN2", target_bir_lowering=False, num_devices=1)
    args = [nc.dram_tensor(k, v.shape, mybir.dt.from_np(v.dtype), kind="ExternalInput").ap() for k, v in arrays.items()]
    out = nc.dram_tensor("outT", (C, N), F32, kind="ExternalOutput").ap()
    build(nc, *args, out)
    r = run_bass_kernel_spmd(nc, [arrays], core_ids=[0])
    return r.results[0]["outT"].T.reshape(BATCH, SEQ, C)
```
